# Optimizing a Trainium2 kernel written in Bass

```python
import numpy as np
import jax
import jax.numpy as jnp

def _softmax(x, axis=-1):
    return jax.nn.softmax(x, axis=axis)

def _gelu(x):
    return jax.nn.gelu(x, approximate=True)

def _silu(x):
    return jax.nn.silu(x)

def _sigmoid(x):
    return jax.nn.sigmoid(x)

def _layernorm(x, axis=-1, eps=1e-05):
    m = jnp.mean(x, axis=axis, keepdims=True)
    v = jnp.var(x, axis=axis, keepdims=True)
    return (x - m) / jnp.sqrt(v + eps)

def _scatter_add(tgt, idx, src, axis=0):
    return tgt.at[idx].add(src)

def _segment_sum(src, seg, n):
    return jax.ops.segment_sum(src, seg, n)
kernel_name = 'mk_conv_preact_d2_conv_nhwc512_r4_f0fdc9'

def setup_inputs(seed: int=0):
    np.random.seed(seed)
    _w = jnp.asarray

    def _rec_inputs():
        import jax
        import jax.numpy as jnp
        _gk = jax.random.key(seed)
        x = 7.22e-05 + 1 * jax.random.normal(jax.random.fold_in(_gk, 1), (4, 16, 16, 128), jnp.float32)
        return x
    x = _rec_inputs()

    def _L0_conv_setup():
        import jax, jax.numpy as jnp
        import numpy as np
        EPS = 1e-07

        def _sum_pool3(x):
            return jax.lax.reduce_window(x, 0.0, jax.lax.add, (1, 3, 3, 1), (1, 1, 1, 1), 'SAME')
        key = jax.random.key(seed)
        k1, k2 = jax.random.split(key)
        B, H, W, C = (4, 16, 16, 128)
        foreground = jax.random.normal(k1, (B, H, W, C), dtype=jnp.float32)
        mask = jnp.ones((B, H, W, 1), dtype=jnp.float32)
        w_comb = jax.random.normal(k2, (2 * C, C), dtype=jnp.float32) * 0.02
        b_comb = jnp.zeros((C,), dtype=jnp.float32)
        return {'foreground': foreground, 'mask': mask, 'w_comb': w_comb, 'b_comb': b_comb}
    _L0_conv_all = _L0_conv_setup()
    _L0_conv_in = {k: v for k, v in _L0_conv_all.items() if k in ('mask', 'w_comb', 'b_comb')}
    del _L0_conv_all

    def _L1_conv_setup():
        import jax, jax.numpy as jnp
        import numpy as np
        EPS = 1e-06
        N_HEADS = 8

        def _proj_heads(x, W, b, N, D):
            B, M, T, C = x.shape
            y = jnp.einsum('bmtc,dc->bmtd', x, W) + b
            return y.reshape(B, M, T, N, D).transpose(0, 1, 3, 2, 4)
        key = jax.random.key(seed)
        ks = jax.random.split(key, 9)
        B, M, T, C = (2, 16, 64, 128)
        s = 0.02
        return {'x': jax.random.normal(ks[0], (B, M, T, C), dtype=jnp.float32), 'Wq': jax.random.normal(ks[1], (C, C), dtype=jnp.float32) * s, 'bq': jnp.zeros((C,), dtype=jnp.float32), 'Wk': jax.random.normal(ks[2], (C, C), dtype=jnp.float32) * s, 'bk': jnp.zeros((C,), dtype=jnp.float32), 'Wv': jax.random.normal(ks[3], (C, C), dtype=jnp.float32) * s, 'bv': jnp.zeros((C,), dtype=jnp.float32), 'Wp': jax.random.normal(ks[4], (C, C), dtype=jnp.float32) * s, 'bp': jnp.zeros((C,), dtype=jnp.float32)}
    _L1_conv_all = _L1_conv_setup()
    _L1_conv_in = {k: v for k, v in _L1_conv_all.items() if k in ('Wq', 'bq', 'Wk', 'bk', 'Wv', 'bv', 'Wp', 'bp')}
    del _L1_conv_all
    return {'x': x, 'L0_conv_mask': _L0_conv_in['mask'], 'L0_conv_w_comb': _L0_conv_in['w_comb'], 'L0_conv_b_comb': _L0_conv_in['b_comb'], 'L1_conv_Wq': _L1_conv_in['Wq'], 'L1_conv_bq': _L1_conv_in['bq'], 'L1_conv_Wk': _L1_conv_in['Wk'], 'L1_conv_bk': _L1_conv_in['bk'], 'L1_conv_Wv': _L1_conv_in['Wv'], 'L1_conv_bv': _L1_conv_in['bv'], 'L1_conv_Wp': _L1_conv_in['Wp'], 'L1_conv_bp': _L1_conv_in['bp']}

def reference(x, L0_conv_mask, L0_conv_w_comb, L0_conv_b_comb, L1_conv_Wq, L1_conv_bq, L1_conv_Wk, L1_conv_bk, L1_conv_Wv, L1_conv_bv, L1_conv_Wp, L1_conv_bp):
    import jax
    import jax.numpy as jnp

    def _L0_conv_ref(foreground, mask, w_comb, b_comb):
        import jax, jax.numpy as jnp
        import numpy as np
        EPS = 1e-07

        def _sum_pool3(x):
            return jax.lax.reduce_window(x, 0.0, jax.lax.add, (1, 3, 3, 1), (1, 1, 1, 1), 'SAME')
        B, H, W, C = foreground.shape
        HW = H * W
        f = foreground.reshape(B, HW, C)
        k = f + EPS
        k = k / jnp.sqrt(jnp.sum(k * k, axis=-1, keepdims=True))
        scores = jnp.einsum('bpc,bqc->bpq', f, k)
        scores = scores.reshape(B, H, W, HW)
        cnt = _sum_pool3(jnp.ones((1, H, W, 1), foreground.dtype))
        scores = _sum_pool3(scores) / cnt * 9.0
        att = jax.nn.softmax(scores, axis=-1)
        recon = jnp.einsum('bpq,bqc->bpc', att.reshape(B, HW, HW), k).reshape(B, H, W, C)
        cat = jnp.concatenate([recon, foreground], axis=-1)
        out = jnp.einsum('bhwc,cd->bhwd', cat, w_comb) + b_comb
        return out

    def _L1_conv_ref(x, Wq, bq, Wk, bk, Wv, bv, Wp, bp):
        import jax, jax.numpy as jnp
        import numpy as np
        EPS = 1e-06
        N_HEADS = 8

        def _proj_heads(x, W, b, N, D):
            B, M, T, C = x.shape
            y = jnp.einsum('bmtc,dc->bmtd', x, W) + b
            return y.reshape(B, M, T, N, D).transpose(0, 1, 3, 2, 4)
        B, M, T, C = x.shape
        N = N_HEADS
        D = C // N
        q = _proj_heads(x, Wq, bq, N, D)
        k = _proj_heads(x, Wk, bk, N, D)
        v = _proj_heads(x, Wv, bv, N, D)
        q = jax.nn.elu(q) + 1.0
        k = jax.nn.elu(k) + 1.0
        KtV = jnp.einsum('bmntd,bmnte->bmnde', k, v)
        ksum = jnp.sum(k, axis=-2)
        z = 1.0 / (jnp.einsum('bmntd,bmnd->bmnt', q, ksum) + EPS)
        KtV_colsum = jnp.sum(KtV, axis=-2)
        V = z[..., None] * KtV_colsum[..., None, :]
        V = V.transpose(0, 1, 3, 2, 4).reshape(B, M, T, N * D)
        out = jnp.einsum('bmtc,dc->bmtd', V, Wp) + bp
        return out

    def _gn(v, G=32, eps=1e-05):
        B_, H_, W_, C_ = v.shape
        g = v.reshape(B_, H_, W_, G, C_ // G)
        m = jnp.mean(g, axis=(1, 2, 4), keepdims=True)
        s = jnp.var(g, axis=(1, 2, 4), keepdims=True)
        return ((g - m) / jnp.sqrt(s + eps)).reshape(v.shape)

    def _ln_c(v, eps=1e-06):
        m = jnp.mean(v, axis=-1, keepdims=True)
        s = jnp.var(v, axis=-1, keepdims=True)
        return (v - m) / jnp.sqrt(s + eps)

    def _ln_t(v, eps=1e-05):
        m = jnp.mean(v, axis=-1, keepdims=True)
        s = jnp.var(v, axis=-1, keepdims=True)
        return (v - m) / jnp.sqrt(s + eps)

    def _to_tokens(v):
        B_, H_, W_, C_ = v.shape
        return v.reshape(B_, H_ * W_, C_)

    def _from_tokens(t, like):
        return t.reshape(like.shape)
    x = x + _L0_conv_ref(_gn(x), L0_conv_mask, L0_conv_w_comb, L0_conv_b_comb)
    x = x + _L1_conv_ref(_gn(x), L1_conv_Wq, L1_conv_bq, L1_conv_Wk, L1_conv_bk, L1_conv_Wv, L1_conv_bv, L1_conv_Wp, L1_conv_bp)
    return x

_drawn_inputs = setup_inputs


def setup_inputs(seed=0):
    import zlib

    import numpy as np

    out = dict(_drawn_inputs(seed))
    spreads = {'L0_conv_b_comb': (0.0, 0.1),
     'L1_conv_bq': (0.0, 0.8),
     'L1_conv_bk': (0.0, 0.8),
     'L1_conv_bv': (0.0, 0.319),
     'L1_conv_bp': (0.0, 0.1)}
    factors = {'L1_conv_Wq': 8.0, 'L1_conv_Wk': 8.0, 'L1_conv_Wv': 4.316}
    for name, (base, spread) in spreads.items():
        noise = np.random.default_rng([zlib.crc32(name.encode()), seed]).standard_normal(out[name].shape)
        drawn = base * np.exp(spread * noise) if base else spread * noise
        out[name] = jnp.asarray(drawn.astype(out[name].dtype))
    for name, factor in factors.items():
        out[name] = (out[name] * factor).astype(out[name].dtype)
    return out
```

```python
import numpy as np

import concourse.bass as bass
from concourse import mybir
from concourse.alu_op_type import AluOpType as ALU
from contextlib import ExitStack

F32 = mybir.dt.float32
BF16 = mybir.dt.bfloat16
ACT = mybir.ActivationFunctionType
AX = mybir.AxisListType

BATCH, H, W, C = 4, 16, 16, 128
TOK = H * W
P = 128
TT = TOK // P
GROUP = C // 32
HEADS = 8
HD = C // HEADS
ROWS = P // W
POOL_COLS = (ROWS + 1) * W
BIAS_ROWS = 96
GN_EPS = 1e-5
KEY_EPS = 1e-7
ATT_EPS = 1e-6

WEIGHTS = {}
for _name, _width in (("w_recon", C), ("w_fore", C), ("wq", C), ("wk", C), ("wv", C), ("wp", C),
                      ("b_comb", 1), ("bp", 1)):
    WEIGHTS[_name] = (sum(w for _, w in WEIGHTS.values()), _width)
WEIGHT_COLS = sum(w for _, w in WEIGHTS.values())

CONSTS = {}
for _name, _width in (("group_mean", P), ("group_rest", P), ("nine", 2), ("blocks", HEADS),
                      ("identity", P), ("window", TT * POOL_COLS)):
    CONSTS[_name] = (sum(w for _, w in CONSTS.values()), _width)
CONST_COLS = sum(w for _, w in CONSTS.values())
STATS_COLS = CONSTS["identity"][0]


def build_block(nc, x_chan, x_tok, consts, weights, bias_rows, out):
    ctx = ExitStack()
    with ctx:
        def sb(name, shape, dt=F32):
            return ctx.enter_context(nc.sbuf_tensor(name, shape, dt))

        def psum(name):
            return ctx.enter_context(nc.psum_tensor(name, [P, 512], F32))

        def sem(name):
            return ctx.enter_context(nc.semaphore(name))

        xT = sb("xT", [P, BATCH, TOK])
        xt = sb("xt", [P, BATCH, TT, C])
        cst = sb("cst", [P, CONST_COLS])
        wts = sb("wts", [P, WEIGHT_COLS])
        bias_in = sb("bias_in", [BIAS_ROWS, 3 * C])
        bias_rest = sb("bias_rest", [BIAS_ROWS, 2, 3 * C])
        bias_parts = sb("bias_parts", [BIAS_ROWS, 3, 3 * C], BF16)
        bias = sb("bias", [BIAS_ROWS, 3 * C], BF16)
        ones = sb("ones", [P, P])
        ones_b = sb("ones_b", [BIAS_ROWS, TOK], BF16)
        eps = sb("eps", [P, 3])

        raw1 = sb("raw1", [P, BATCH, 6])
        chan1 = sb("chan1", [P, BATCH, 2])
        spread1 = sb("spread1", [P, BATCH])
        mean1 = sb("mean1", [P, BATCH, 2])
        lnvar1 = sb("lnvar1", [P, BATCH])
        rstd1 = sb("rstd1", [P, BATCH])
        fT = sb("fT", [P, BATCH, TOK])
        fpT = sb("fpT", [P, BATCH, TOK])
        sqT = sb("sqT", [P, BATCH, TOK])
        lnorm = sb("lnorm", [P, BATCH, TOK])
        rnorm = sb("rnorm", [P, BATCH, TOK])
        kT = sb("kT", [P, BATCH, TOK])
        kw = sb("kw", [P, BATCH, TT, C])
        negmax = sb("negmax", [P, BATCH, TT])
        esum = sb("esum", [P, BATCH, TT])
        rsum = sb("rsum", [P, BATCH, TT])
        e = sb("e", [P, BATCH, TT, TOK])
        att = sb("att", [P, BATCH, TT, TOK])
        attT = sb("attT", [P, BATCH, TT, TOK])
        x1T = sb("x1T", [P, BATCH, TOK])

        raw2 = sb("raw2", [P, BATCH, 6])
        chan2 = sb("chan2", [P, BATCH, 2])
        spread2 = sb("spread2", [P, BATCH])
        mean2 = sb("mean2", [P, BATCH])
        lnvar2 = sb("lnvar2", [P, BATCH])
        rstd2 = sb("rstd2", [P, BATCH])
        gT = sb("gT", [P, BATCH, TOK])
        eqk = sb("eqk", [P, BATCH, 2 * TOK])
        phi = sb("phi", [P, BATCH, 2 * TOK])
        kd = sb("kd", [P, BATCH, TT * HEADS])
        kv = sb("kv", [P, BATCH, TT, C])
        sums = sb("sums", [P, BATCH, 2, H])
        qk = sb("qk", [P, BATCH, TOK])
        den = sb("den", [P, BATCH, TT * HEADS])
        z = sb("z", [P, BATCH, TT * HEADS])
        zc = sb("zc", [P, BATCH, TT, C])
        vT = sb("vT", [P, BATCH, TOK])
        yT = sb("yT", [P, BATCH, TOK])

        ps_pool = psum("ps_pool")
        ps_key = psum("ps_key")
        ps_score = psum("ps_score")
        ps_attT = psum("ps_attT")
        ps_mix = psum("ps_mix")
        ps_qk = psum("ps_qk")
        ps_v = psum("ps_v")
        ps_out = psum("ps_out")
        POOLED = ps_pool[:, 0:TOK]
        MEAN1, REST1, VAR1 = (ps_pool[:, TOK + i:TOK + i + 1] for i in range(3))
        NORM2 = ps_key[:, 0:TOK]
        KW = ps_key[:, TOK:2 * TOK]
        SCORE = ps_score[:, :].rearrange("p (t q) -> p t q", t=TT)
        ATTT = ps_attT[:, :].rearrange("p (t q) -> p t q", t=TT)
        MIX = ps_mix[:, 0:TOK]
        MEAN2, REST2, VAR2 = (ps_mix[:, TOK + i:TOK + i + 1] for i in range(3))
        Q1 = ps_qk[:, 0:TOK]
        K1 = ps_qk[:, TOK:2 * TOK]
        V = ps_v[:, 0:TOK]
        SUMS = ps_v[:, TOK:TOK + 2 * H]
        DEN = ps_v[:, TOK + 2 * H:TOK + 2 * H + TT * HEADS]
        ZT = ps_out[:, 0:TOK]
        OUT = ps_out[:, TOK:2 * TOK]

        def weight(name):
            a, n = WEIGHTS[name]
            return wts[:, a:a + n]

        def const(name):
            a, n = CONSTS[name]
            return cst[:, a:a + n]

        x_chan_in = [sem(f"x_chan_in{b}") for b in range(BATCH)]
        x_tok_in = [sem(f"x_tok_in{b}") for b in range(BATCH)]
        stats_consts_in, consts_in, weights_in, bias_in_sem = (
            sem("stats_consts_in"), sem("consts_in"), sem("weights_in"), sem("bias_in_sem"))
        ones_set, ones_b_set, eps_set = sem("ones_set"), sem("ones_b_set"), sem("eps_set")
        bias_split, bias_ready = sem("bias_split"), sem("bias_ready")
        raw1_done, chan1_done, centre1_done, mean1_done, spread1_done, var1_done, ln1_done, rstd1_done = (
            sem(n) for n in ("raw1_done", "chan1_done", "centre1_done", "mean1_done", "spread1_done",
                             "var1_done", "ln1_done", "rstd1_done"))
        pooled_done, f_done, fp_done, sq_done, norm2_done, lnorm_done, rnorm_done, key_done = (
            sem(n) for n in ("pooled_done", "f_done", "fp_done", "sq_done", "norm2_done", "lnorm_done",
                             "rnorm_done", "key_done"))
        score_done, kw_done, kw_copied, max_done, exp_done, rsum_done, att_done, attT_done, attT_copied = (
            sem(n) for n in ("score_done", "kw_done", "kw_copied", "max_done", "exp_done", "rsum_done",
                             "att_done", "attT_done", "attT_copied"))
        mix_done, x1_done = sem("mix_done"), sem("x1_done")
        raw2_done, chan2_done, centre2_done, mean2_done, spread2_done, var2_done, ln2_done, rstd2_done = (
            sem(n) for n in ("raw2_done", "chan2_done", "centre2_done", "mean2_done", "spread2_done",
                             "var2_done", "ln2_done", "rstd2_done"))
        g_done, qk_proj_done, v_proj_done, eqk_done, phi_done, kd_done, kv_done, sums_done, sums_copied = (
            sem(n) for n in ("g_done", "qk_proj_done", "v_proj_done", "eqk_done", "phi_done", "kd_done",
                             "kv_done", "sums_done", "sums_copied"))
        qk_done, den_done, den_read, z_done, zc_done, zT_done, vT_done, out_done, y_done, stored = (
            sem(n) for n in ("qk_done", "den_done", "den_read", "z_done", "zc_done", "zT_done", "vT_done", "out_done",
                             "y_done", "stored"))

        def interleave(steps, skew):
            last = max(tick for tick, _ in steps) + skew * (BATCH - 1)
            for now in range(last + 1):
                for tick, step in steps:
                    b, rest = divmod(now - tick, skew)
                    if rest == 0 and 0 <= b < BATCH:
                        step(b)

        SKEW = 12

        block = ctx.enter_context(nc.Block())

        @block.sync
        def _(sp):
            sp.dma_start(xT[:, 0, :], x_chan[:, 0, :]).then_inc(x_chan_in[0], 16)
            sp.dma_start(xt[:, 0], x_tok[:, 0]).then_inc(x_tok_in[0], 16)
            for b in range(1, BATCH):
                sp.dma_start(xT[:, b, :], x_chan[:, b, :]).then_inc(x_chan_in[b], 16)
                sp.dma_start(xt[:, b], x_tok[:, b]).then_inc(x_tok_in[b], 16)
            for b in range(BATCH):
                sp.wait_ge(y_done, b + 1)
                sp.dma_start(out[b], yT[:, b, :]).then_inc(stored, 16)
            sp.wait_ge(stored, 16 * BATCH)

        @block.gpsimd
        def _(pool):
            nc.gpsimd.memset(ones[:, :], 1.0).then_inc(ones_set, 1)
            pool.dma_start(wts[:, :], weights).then_inc(weights_in, 16)
            pool.dma_start(bias_in[:, :], bias_rows).then_inc(bias_in_sem, 16)
            nc.gpsimd.memset(ones_b[:, :], 1.0).then_inc(ones_b_set, 1)

            def normalise(b):
                pool.wait_ge(exp_done, TT * (b + 1))
                pool.wait_ge(rsum_done, b + 1)
                for t in range(TT):
                    nc.gpsimd.tensor_scalar(att[:, b, t, :], e[:, b, t, :], rsum[:, b, t:t + 1], None,
                                            ALU.mult).then_inc(att_done, 1)

            def query_times_sums(b):
                pool.wait_ge(phi_done, b + 1)
                pool.wait_ge(sums_copied, b + 1)
                nc.gpsimd.tensor_tensor(
                    qk[:, b, :].rearrange("p (h w) -> p h w", w=W),
                    phi[:, b, 0:TOK].rearrange("p (h w) -> p h w", w=W),
                    sums[:, b, 0, :].unsqueeze(2).to_broadcast([P, H, W]), ALU.mult).then_inc(qk_done, 1)

            interleave([(9, normalise), (22, query_times_sums)], SKEW)

        @block.scalar
        def _(act):
            act.dma_start(cst[:, 0:STATS_COLS], consts[:, 0:STATS_COLS]).then_inc(stats_consts_in, 16)
            act.dma_start(cst[:, STATS_COLS:], consts[:, STATS_COLS:]).then_inc(consts_in, 16)
            nc.scalar.preload_act_table_set("natural_log_exp_and_others")
            act.wait_ge(eps_set, 3)

            def rstd_first(b):
                act.wait_ge(var1_done, b + 1)
                nc.scalar.activation(lnvar1[:, b:b + 1], VAR1, ACT.Ln, bias=eps[:, 0:1]).then_inc(ln1_done, 1)
                act.wait_ge(ln1_done, b + 1)
                nc.scalar.activation(rstd1[:, b:b + 1], lnvar1[:, b:b + 1], ACT.Exp,
                                     scale=-0.5).then_inc(rstd1_done, 1)

            def squares(b):
                act.wait_ge(f_done, b + 1)
                nc.scalar.activation(sqT[:, b, :], fT[:, b, :], ACT.Square, bias=eps[:, 1:2]).then_inc(sq_done, 1)

            def key_scale(b):
                act.wait_ge(norm2_done, b + 1)
                nc.scalar.activation(lnorm[:, b, :], NORM2, ACT.Ln).then_inc(lnorm_done, 1)
                act.wait_ge(lnorm_done, b + 1)
                nc.scalar.activation(rnorm[:, b, :], lnorm[:, b, :], ACT.Exp, scale=-0.5).then_inc(rnorm_done, 1)

            def exponentials(b):
                act.wait_ge(max_done, b + 1)
                for t in range(TT):
                    nc.scalar.activation(e[:, b, t, :], SCORE[:, t, :], ACT.Exp, bias=negmax[:, b, t:t + 1],
                                         accum_out=esum[:, b, t:t + 1]).then_inc(exp_done, 1)

            def copy_kw(b):
                act.wait_ge(kw_done, b + 1)
                nc.scalar.copy(kw[:, b].rearrange("p t c -> p (t c)"), KW).then_inc(kw_copied, 1)

            def copy_attT(b):
                act.wait_ge(attT_done, b + 1)
                nc.scalar.copy(attT[:, b].rearrange("p t q -> p (t q)"), ps_attT[:, :]).then_inc(attT_copied, 1)

            def rstd_second(b):
                act.wait_ge(var2_done, b + 1)
                nc.scalar.activation(lnvar2[:, b:b + 1], VAR2, ACT.Ln, bias=eps[:, 0:1]).then_inc(ln2_done, 1)
                act.wait_ge(ln2_done, b + 1)
                nc.scalar.activation(rstd2[:, b:b + 1], lnvar2[:, b:b + 1], ACT.Exp,
                                     scale=-0.5).then_inc(rstd2_done, 1)

            def exp_qk(b):
                act.wait_ge(qk_proj_done, b + 1)
                nc.scalar.activation(eqk[:, b, :], ps_qk[:, :], ACT.Exp, bias=eps[:, 2:3]).then_inc(eqk_done, 1)

            def copy_sums(b):
                act.wait_ge(sums_done, b + 1)
                nc.scalar.copy(sums[:, b].rearrange("p s h -> p (s h)"), SUMS).then_inc(sums_copied, 1)

            def widen_reciprocals(b):
                act.wait_ge(z_done, b + 1)
                nc.scalar.copy(zc[:, b].rearrange("p t (n d) -> p (t n) d", d=HD),
                               z[:, b, :].unsqueeze(2).to_broadcast([P, TT * HEADS, HD])).then_inc(zc_done, 1)

            interleave([(23, widen_reciprocals), (2, rstd_first), (3, squares), (5, key_scale), (7, exponentials), (8, copy_kw),
                        (11, copy_attT), (15, rstd_second), (18, exp_qk), (21, copy_sums)], SKEW)

        @block.vector
        def _(dve):
            for i, value in enumerate((GN_EPS, KEY_EPS, -1.0)):
                nc.vector.memset(eps[:, i:i + 1], value).then_inc(eps_set, 1)

            def split_biases():
                dve.wait_ge(bias_in_sem, 16)
                nc.vector.tensor_copy(bias_parts[:, 0, :], bias_in[:, :]).then_inc(bias_split, 1)
                dve.wait_ge(bias_split, 1)
                nc.vector.tensor_tensor(bias_rest[:, 0, :], bias_in[:, :], bias_parts[:, 0, :],
                                        ALU.subtract).then_inc(bias_split, 1)
                dve.wait_ge(bias_split, 2)
                nc.vector.tensor_copy(bias_parts[:, 1, :], bias_rest[:, 0, :]).then_inc(bias_split, 1)
                dve.wait_ge(bias_split, 3)
                nc.vector.tensor_tensor(bias_rest[:, 1, :], bias_rest[:, 0, :], bias_parts[:, 1, :],
                                        ALU.subtract).then_inc(bias_split, 1)
                dve.wait_ge(bias_split, 4)
                nc.vector.tensor_copy(bias_parts[:, 2, :], bias_rest[:, 1, :]).then_inc(bias_split, 1)
                dve.wait_ge(bias_split, 5)
                for i in range(3):
                    nc.vector.tensor_copy(bias[32 * i:32 * i + 32, :],
                                          bias_parts[32 * i:32 * i + 32, i, :]).then_inc(bias_ready, 1)

            def channel_stats_first(b):
                dve.wait_ge(x_chan_in[b], 16)
                nc.vector.bn_stats(raw1[:, b, :], xT[:, b, :]).then_inc(raw1_done, 1)
                dve.wait_ge(raw1_done, b + 1)
                nc.vector.bn_aggr(chan1[:, b, :], raw1[:, b, :]).then_inc(chan1_done, 1)

            def group_stats_first(b):
                if b == 0:
                    dve.wait_ge(stats_consts_in, 16)
                dve.wait_ge(centre1_done, b + 1)
                nc.vector.scalar_tensor_tensor(spread1[:, b:b + 1], REST1, REST1, chan1[:, b, 1:2],
                                               ALU.mult, ALU.add).then_inc(spread1_done, 1)
                nc.vector.tensor_scalar(mean1[:, b, :], const("nine"), MEAN1, None,
                                        ALU.mult).then_inc(mean1_done, 1)

            def normalise_first(b):
                dve.wait_ge(rstd1_done, b + 1)
                dve.wait_ge(mean1_done, b + 1)
                nc.vector.tensor_scalar(fT[:, b, :], xT[:, b, :], mean1[:, b, 0:1], rstd1[:, b:b + 1],
                                        ALU.subtract, ALU.mult).then_inc(f_done, 1)
                dve.wait_ge(pooled_done, b + 1)
                nc.vector.tensor_scalar(fpT[:, b, :], POOLED, mean1[:, b, 1:2], rstd1[:, b:b + 1],
                                        ALU.subtract, ALU.mult).then_inc(fp_done, 1)

            def keys(b):
                dve.wait_ge(rnorm_done, b + 1)
                dve.wait_ge(f_done, b + 1)
                nc.vector.scalar_tensor_tensor(kT[:, b, :], fT[:, b, :], KEY_EPS, rnorm[:, b, :],
                                               ALU.add, ALU.mult).then_inc(key_done, 1)

            def row_max(b):
                dve.wait_ge(score_done, b + 1)
                nc.vector.tensor_reduce(negmax[:, b, :], SCORE, AX.X, ALU.max, negate=True).then_inc(max_done, 1)

            def row_sum(b):
                dve.wait_ge(exp_done, TT * (b + 1))
                nc.vector.reciprocal(rsum[:, b, :], esum[:, b, :]).then_inc(rsum_done, 1)

            def first_residual(b):
                if b == 0:
                    dve.wait_ge(weights_in, 16)
                dve.wait_ge(mix_done, b + 1)
                nc.vector.scalar_tensor_tensor(x1T[:, b, :], MIX, weight("b_comb"), xT[:, b, :],
                                               ALU.add, ALU.add).then_inc(x1_done, 1)
                dve.wait_ge(x1_done, b + 1)
                nc.vector.bn_stats(raw2[:, b, :], x1T[:, b, :]).then_inc(raw2_done, 1)
                dve.wait_ge(raw2_done, b + 1)
                nc.vector.bn_aggr(chan2[:, b, :], raw2[:, b, :]).then_inc(chan2_done, 1)

            def group_stats_second(b):
                dve.wait_ge(centre2_done, b + 1)
                nc.vector.scalar_tensor_tensor(spread2[:, b:b + 1], REST2, REST2, chan2[:, b, 1:2],
                                               ALU.mult, ALU.add).then_inc(spread2_done, 1)
                nc.vector.tensor_copy(mean2[:, b:b + 1], MEAN2).then_inc(mean2_done, 1)

            def normalise_second(b):
                dve.wait_ge(rstd2_done, b + 1)
                dve.wait_ge(mean2_done, b + 1)
                nc.vector.tensor_scalar(gT[:, b, :], x1T[:, b, :], mean2[:, b:b + 1], rstd2[:, b:b + 1],
                                        ALU.subtract, ALU.mult).then_inc(g_done, 1)

            def feature_map(b):
                dve.wait_ge(eqk_done, b + 1)
                nc.vector.scalar_tensor_tensor(phi[:, b, :], eqk[:, b, :], 1.0, ps_qk[:, :],
                                               ALU.min, ALU.max).then_inc(phi_done, 1)
                dve.wait_ge(phi_done, b + 1)
                nc.vector.tensor_reduce(kd[:, b, :], phi[:, b, TOK:].rearrange("p (n d) -> p n d", d=HD),
                                        AX.X, ALU.add).then_inc(kd_done, 1)
                dve.wait_ge(kd_done, b + 1)
                dve.wait_ge(v_proj_done, b + 1)
                nc.vector.tensor_tensor(
                    kv[:, b].rearrange("p t (n d) -> p (t n) d", d=HD), V.rearrange("p (n d) -> p n d", d=HD),
                    kd[:, b, :].unsqueeze(2).to_broadcast([P, TT * HEADS, HD]), ALU.mult).then_inc(kv_done, 1)

            def reciprocals(b):
                dve.wait_ge(den_done, b + 1)
                nc.vector.tensor_scalar(den[:, b, :], DEN, ATT_EPS, None, ALU.add).then_inc(den_read, 1)
                dve.wait_ge(den_read, b + 1)
                nc.vector.reciprocal(z[:, b, :], den[:, b, :]).then_inc(z_done, 1)

            def attended(b):
                dve.wait_ge(zT_done, b + 1)
                dve.wait_ge(sums_copied, b + 1)
                nc.vector.tensor_tensor(
                    vT[:, b, :].rearrange("p (h w) -> p h w", w=W), ZT.rearrange("p (h w) -> p h w", w=W),
                    sums[:, b, 1, :].unsqueeze(2).to_broadcast([P, H, W]), ALU.mult).then_inc(vT_done, 1)

            def second_residual(b):
                dve.wait_ge(out_done, b + 1)
                nc.vector.scalar_tensor_tensor(yT[:, b, :], OUT, weight("bp"), x1T[:, b, :],
                                               ALU.add, ALU.add).then_inc(y_done, 1)

            channel_stats_first(0)
            group_stats_first(0)
            split_biases()
            interleave([(0, lambda b: channel_stats_first(b) if b else None),
                        (1, lambda b: group_stats_first(b) if b else None),
                        (3, normalise_first), (5, keys), (7, row_max), (9, row_sum), (13, first_residual),
                        (14, group_stats_second), (16, normalise_second), (19, feature_map),
                        (23, reciprocals), (24, attended), (26, second_residual)], SKEW)

        @block.tensor
        def _(pe):
            def window_sums(b):
                if b == 0:
                    pe.wait_ge(consts_in, 16)
                pe.wait_ge(x_tok_in[b], 16)
                pe.wait_ge(ln1_done, b + 1)
                for t in range(TT):
                    first = t * (TOK - POOL_COLS)
                    mm = nc.tensor.matmul(POOLED[:, first:first + POOL_COLS], xt[:, b, t, :],
                                          const("window")[:, t * POOL_COLS:(t + 1) * POOL_COLS],
                                          start=(t == 0), stop=(t == TT - 1), skip_group_check=True)
                mm.then_inc(pooled_done, 1)

            def group_centre_first(b):
                if b == 0:
                    pe.wait_ge(stats_consts_in, 16)
                pe.wait_ge(chan1_done, b + 1)
                if b >= 1:
                    pe.wait_ge(fp_done, b)
                nc.tensor.matmul(MEAN1, const("group_mean"), chan1[:, b, 0:1], start=True, stop=True)
                nc.tensor.matmul(REST1, const("group_rest"), chan1[:, b, 0:1],
                                 start=True, stop=True).then_inc(centre1_done, 1)

            def group_var_first(b):
                pe.wait_ge(spread1_done, b + 1)
                pe.wait_ge(mean1_done, b + 1)
                nc.tensor.matmul(VAR1, const("group_mean"), spread1[:, b:b + 1],
                                 start=True, stop=True).then_inc(var1_done, 1)

            def key_norms(b):
                if b == 0:
                    pe.wait_ge(ones_set, 1)
                pe.wait_ge(sq_done, b + 1)
                if b >= 1:
                    pe.wait_ge(kw_copied, b)
                nc.tensor.matmul(NORM2, ones[:, :], sqT[:, b, :], start=True, stop=True).then_inc(norm2_done, 1)

            def scores(b):
                pe.wait_ge(key_done, b + 1)
                pe.wait_ge(fp_done, b + 1)
                if b >= 1:
                    pe.wait_ge(exp_done, TT * b)
                for t in range(TT):
                    mm = nc.tensor.matmul(SCORE[:, t, :], fpT[:, b, t * P:(t + 1) * P], kT[:, b, :],
                                          start=True, stop=True)
                mm.then_inc(score_done, 1)

            def keys_recon(b):
                if b == 0:
                    pe.wait_ge(weights_in, 16)
                pe.wait_ge(lnorm_done, b + 1)
                for t in range(TT):
                    mm = nc.tensor.matmul(KW[:, t * C:(t + 1) * C], kT[:, b, t * P:(t + 1) * P],
                                          weight("w_recon"), start=True, stop=True)
                mm.then_inc(kw_done, 1)

            def transpose_att(b):
                if b >= 1:
                    pe.wait_ge(attT_copied, b)
                for t in range(TT):
                    pe.wait_ge(att_done, TT * b + t + 1)
                    for s in range(TT):
                        mm = nc.tensor.transpose(ATTT[:, s, t * P:(t + 1) * P],
                                                 att[:, b, t, s * P:(s + 1) * P], const("identity"))
                mm.then_inc(attT_done, 1)

            def mix(b):
                if b >= 1:
                    pe.wait_ge(rstd2_done, b)
                    pe.wait_ge(mean2_done, b)
                nc.tensor.matmul(MIX, weight("w_fore"), fT[:, b, :], start=True, stop=False)
                pe.wait_ge(kw_copied, b + 1)
                pe.wait_ge(attT_copied, b + 1)
                for t in range(TT):
                    mm = nc.tensor.matmul(MIX, kw[:, b, t, :], attT[:, b, t, :], start=False, stop=(t == TT - 1))
                mm.then_inc(mix_done, 1)

            def group_centre_second(b):
                pe.wait_ge(chan2_done, b + 1)
                nc.tensor.matmul(MEAN2, const("group_mean"), chan2[:, b, 0:1], start=True, stop=True)
                nc.tensor.matmul(REST2, const("group_rest"), chan2[:, b, 0:1],
                                 start=True, stop=True).then_inc(centre2_done, 1)

            def group_var_second(b):
                pe.wait_ge(spread2_done, b + 1)
                pe.wait_ge(mean2_done, b + 1)
                nc.tensor.matmul(VAR2, const("group_mean"), spread2[:, b:b + 1],
                                 start=True, stop=True).then_inc(var2_done, 1)

            def projections(b):
                if b == 0:
                    pe.wait_ge(ones_b_set, 1)
                    pe.wait_ge(bias_ready, 3)
                pe.wait_ge(g_done, b + 1)
                if b >= 1:
                    pe.wait_ge(phi_done, b)
                nc.tensor.matmul(Q1, weight("wq"), gT[:, b, :], start=True, stop=False)
                nc.tensor.matmul(Q1, bias[:, 0:C], ones_b[:, :], start=False, stop=True)
                for t in range(TT):
                    out_k = K1[:, t * C:(t + 1) * C]
                    nc.tensor.matmul(out_k, gT[:, b, t * P:(t + 1) * P], weight("wk"), start=True, stop=False)
                    mm = nc.tensor.matmul(out_k, ones_b[:, 0:P], bias[:, C:2 * C], start=False, stop=True)
                mm.then_inc(qk_proj_done, 1)
                if b >= 1:
                    pe.wait_ge(den_read, b)
                for t in range(TT):
                    out_v = V[:, t * C:(t + 1) * C]
                    nc.tensor.matmul(out_v, gT[:, b, t * P:(t + 1) * P], weight("wv"), start=True, stop=False)
                    mm = nc.tensor.matmul(out_v, ones_b[:, 0:P], bias[:, 2 * C:3 * C], start=False, stop=True)
                mm.then_inc(v_proj_done, 1)

            def row_sums(b):
                pe.wait_ge(kv_done, b + 1)
                pe.wait_ge(phi_done, b + 1)
                for t in range(TT):
                    nc.tensor.matmul(SUMS[:, t * ROWS:(t + 1) * ROWS],
                                     phi[:, b, TOK + t * C:TOK + (t + 1) * C], const("blocks"),
                                     start=True, stop=True)
                    mm = nc.tensor.matmul(SUMS[:, H + t * ROWS:H + (t + 1) * ROWS], kv[:, b, t, :],
                                          const("blocks"), start=True, stop=True)
                mm.then_inc(sums_done, 1)

            def denominators(b):
                pe.wait_ge(qk_done, b + 1)
                for t in range(TT):
                    mm = nc.tensor.matmul(DEN[:, t * HEADS:(t + 1) * HEADS], qk[:, b, t * P:(t + 1) * P],
                                          const("blocks"), start=True, stop=True)
                mm.then_inc(den_done, 1)

            def spread_reciprocals(b):
                pe.wait_ge(zc_done, b + 1)
                if b >= 1:
                    pe.wait_ge(y_done, b)
                for t in range(TT):
                    mm = nc.tensor.transpose(ZT[:, t * P:(t + 1) * P], zc[:, b, t, :], const("identity"))
                mm.then_inc(zT_done, 1)

            def output_projection(b):
                pe.wait_ge(vT_done, b + 1)
                nc.tensor.matmul(OUT, weight("wp"), vT[:, b, :], start=True, stop=True).then_inc(out_done, 1)

            interleave([(0, group_centre_first), (1, group_var_first), (2, window_sums), (4, key_norms),
                        (6, scores), (7, keys_recon), (10, transpose_att), (12, mix),
                        (14, group_centre_second), (15, group_var_second), (17, projections),
                        (20, row_sums), (22, denominators), (23, spread_reciprocals),
                        (25, output_projection)], SKEW)


def shape_constants():
    eye = np.eye(P, dtype=np.float32)
    same_group = np.kron(np.eye(P // GROUP, dtype=np.float32), np.ones((GROUP, GROUP), np.float32)) / GROUP
    nine = np.tile(np.array([[1.0, 9.0]], np.float32), (P, 1))
    blocks = np.kron(np.eye(HEADS, dtype=np.float32), np.ones((HD, 1), np.float32))
    near = (np.abs(np.subtract.outer(np.arange(H), np.arange(H))) <= 1).astype(np.float32)
    line = near / near.sum(0) * 3.0
    full = np.kron(line, line)
    window = [full[t * P:(t + 1) * P, t * (TOK - POOL_COLS):t * (TOK - POOL_COLS) + POOL_COLS] for t in range(TT)]
    return np.ascontiguousarray(
        np.concatenate([same_group, eye - same_group, nine, blocks, eye] + window, axis=1).astype(np.float32))


def kernel(x, L0_conv_mask, L0_conv_w_comb, L0_conv_b_comb, L1_conv_Wq, L1_conv_bq, L1_conv_Wk, L1_conv_bk,
           L1_conv_Wv, L1_conv_bv, L1_conv_Wp, L1_conv_bp):
    import concourse.bacc as bacc
    from concourse.bass_utils import run_bass_kernel_spmd

    images = np.asarray(x).reshape(BATCH, TOK, C)
    w_comb = np.asarray(L0_conv_w_comb)
    bias_rows = np.zeros((BIAS_ROWS, 3 * C), np.float32)
    for part in range(3):
        for i, row in enumerate((L1_conv_bq, L1_conv_bk, L1_conv_bv)):
            bias_rows[32 * part, i * C:(i + 1) * C] = np.asarray(row)
    bias_rows[1, 0:2 * C] = 1.0
    arrays = {
        "x_chan": np.ascontiguousarray(images.transpose(2, 0, 1)),
        "x_tok": np.ascontiguousarray(images.reshape(BATCH, TT, P, C).transpose(2, 0, 1, 3)),
        "consts": shape_constants(),
        "weights": np.ascontiguousarray(np.concatenate(
            [w_comb[0:C], w_comb[C:2 * C], np.asarray(L1_conv_Wq).T, np.asarray(L1_conv_Wk).T,
             np.asarray(L1_conv_Wv).T, np.asarray(L1_conv_Wp).T,
             np.asarray(L0_conv_b_comb)[:, None], np.asarray(L1_conv_bp)[:, None]], axis=1)),
        "bias_rows": bias_rows,
    }
    nc = bacc.Bacc("TRN2", target_bir_lowering=False, num_devices=1)
    args = [nc.dram_tensor(name, a.shape, F32, kind="ExternalInput").ap() for name, a in arrays.items()]
    out = nc.dram_tensor("out", (BATCH, C, TOK), F32, kind="ExternalOutput").ap()
    build_block(nc, *args, out)
    got = run_bass_kernel_spmd(nc, [arrays], core_ids=[0]).results[0]["out"]
    return np.ascontiguousarray(got.transpose(0, 2, 1)).reshape(BATCH, H, W, C)
```

```python
import numpy as np

import concourse.bass as bass
from concourse import mybir
from concourse.alu_op_type import AluOpType as ALU
from contextlib import ExitStack

F32 = mybir.dt.float32
BF16 = mybir.dt.bfloat16
ACT = mybir.ActivationFunctionType
AX = mybir.AxisListType

BATCH, H, W, C = 4, 16, 16, 128
TOK = H * W
P = 128
TT = TOK // P
GROUP = C // 32
HEADS = 8
HD = C // HEADS
ROWS = P // W
POOL_COLS = (ROWS + 1) * W
BIAS_ROWS = 96
GN_EPS = 1e-5
KEY_EPS = 1e-7
ATT_EPS = 1e-6

WEIGHTS = {}
for _name, _width in (("w_recon", C), ("w_fore", C), ("wq", C), ("wk", C), ("wv", C), ("wp", C),
                      ("b_comb", 1), ("bp", 1)):
    WEIGHTS[_name] = (sum(w for _, w in WEIGHTS.values()), _width)
WEIGHT_COLS = sum(w for _, w in WEIGHTS.values())

CONSTS = {}
for _name, _width in (("group_mean", P), ("signs", 2 * BATCH), ("blocks", HEADS),
                      ("identity", P), ("window", TT * POOL_COLS)):
    CONSTS[_name] = (sum(w for _, w in CONSTS.values()), _width)
CONST_COLS = sum(w for _, w in CONSTS.values())
STATS_COLS = CONSTS["identity"][0]


def build_block(nc, x_chan, x_tok, consts, weights, bias_rows, out):
    ctx = ExitStack()
    with ctx:
        def sb(name, shape, dt=F32):
            return ctx.enter_context(nc.sbuf_tensor(name, shape, dt))

        def psum(name):
            return ctx.enter_context(nc.psum_tensor(name, [P, 512], F32))

        def sem(name):
            return ctx.enter_context(nc.semaphore(name))

        xT = sb("xT", [P, BATCH, TOK])
        xt = sb("xt", [P, BATCH, TT, C])
        cst = sb("cst", [P, CONST_COLS])
        wts = sb("wts", [P, WEIGHT_COLS])
        bias_in = sb("bias_in", [BIAS_ROWS, 3 * C])
        bias_rest = sb("bias_rest", [BIAS_ROWS, 2, 3 * C])
        bias_parts = sb("bias_parts", [BIAS_ROWS, 3, 3 * C], BF16)
        bias = sb("bias", [BIAS_ROWS, 3 * C], BF16)
        ones = sb("ones", [P, P])
        ones_b = sb("ones_b", [BIAS_ROWS, TOK], BF16)
        eps = sb("eps", [P, 3])

        raw1 = sb("raw1", [P, BATCH, 6])
        chan1 = sb("chan1", [P, BATCH, 2])
        rest1 = sb("rest1", [P, BATCH])
        spread1 = sb("spread1", [P, BATCH])
        mean1 = sb("mean1", [P, 2, BATCH])
        key_bias = sb("key_bias", [P, BATCH])
        lnvar1 = sb("lnvar1", [P, BATCH])
        rstd1 = sb("rstd1", [P, BATCH])
        fT = sb("fT", [P, BATCH, TOK])
        fpT = sb("fpT", [P, BATCH, TOK])
        sqT = sb("sqT", [P, BATCH, TOK])
        lnorm = sb("lnorm", [P, BATCH, TOK])
        rnorm = sb("rnorm", [P, BATCH, TOK])
        kT = sb("kT", [P, BATCH, TOK])
        kw = sb("kw", [P, BATCH, TT, C])
        negmax = sb("negmax", [P, BATCH, TT])
        esum = sb("esum", [P, BATCH, TT])
        rsum = sb("rsum", [P, BATCH, TT])
        e = sb("e", [P, BATCH, TT, TOK])
        att = sb("att", [P, BATCH, TT, TOK])
        attT = sb("attT", [P, BATCH, TT, TOK])
        base = sb("base", [P, BATCH, TOK])
        x1T = sb("x1T", [P, BATCH, TOK])

        raw2 = sb("raw2", [P, BATCH, 6])
        chan2 = sb("chan2", [P, BATCH, 2])
        rest2 = sb("rest2", [P, BATCH])
        spread2 = sb("spread2", [P, BATCH])
        mean2 = sb("mean2", [P, BATCH])
        lnvar2 = sb("lnvar2", [P, BATCH])
        rstd2 = sb("rstd2", [P, BATCH])
        gT = sb("gT", [P, BATCH, TOK])
        ek = sb("ek", [P, BATCH, TOK])
        eq = sb("eq", [P, BATCH, TOK])
        phi_k = sb("phi_k", [P, BATCH, TOK])
        phi_q = sb("phi_q", [P, BATCH, TOK])
        kd = sb("kd", [P, BATCH, TT * HEADS])
        kv = sb("kv", [P, BATCH, TT, C])
        vsum = sb("vsum", [P, BATCH, H])
        qk = sb("qk", [P, BATCH, TOK])
        den = sb("den", [P, BATCH, TT * HEADS])
        z = sb("z", [P, BATCH, TT * HEADS])
        zc = sb("zc", [P, BATCH, TT, C])
        vT = sb("vT", [P, BATCH, TOK])
        yT = sb("yT", [P, BATCH, TOK])

        ps_pool = psum("ps_pool")
        ps_key = psum("ps_key")
        ps_score = psum("ps_score")
        ps_attT = psum("ps_attT")
        ps_mix = psum("ps_mix")
        ps_qk = psum("ps_qk")
        ps_v = psum("ps_v")
        ps_out = psum("ps_out")
        POOLED = [bank[:, 0:TOK] for bank in (ps_pool, ps_qk, ps_v, ps_out)]
        BASE = POOLED
        MEAN1, VAR1 = (ps_mix[:, TOK + BATCH * i:TOK + BATCH * (i + 1)] for i in range(2))
        NORM2 = ps_key[:, 0:TOK]
        KW = ps_key[:, TOK:2 * TOK]
        SCORE = ps_score[:, :].rearrange("p (t q) -> p t q", t=TT)
        ATTT = ps_attT[:, :].rearrange("p (t q) -> p t q", t=TT)
        MIX = ps_mix[:, 0:TOK]
        MEAN2, VAR2 = (ps_qk[:, TOK + i:TOK + i + 1] for i in range(2))
        K1 = ps_pool[:, 0:TOK]
        KSUM = ps_pool[:, TOK:TOK + H]
        Q1 = ps_qk[:, 0:TOK]
        V = ps_v[:, 0:TOK]
        VSUM = ps_v[:, TOK:TOK + H]
        DEN = ps_v[:, TOK + H:TOK + H + TT * HEADS]
        ZT = ps_out[:, 0:TOK]
        OUT = ps_out[:, TOK:2 * TOK]

        def part(b):
            return slice(0, 1) if b == 0 else slice(1, BATCH)

        def weight(name):
            a, n = WEIGHTS[name]
            return wts[:, a:a + n]

        def const(name):
            a, n = CONSTS[name]
            return cst[:, a:a + n]

        x_chan_in = [sem(f"x_chan_in{b}") for b in range(BATCH)]
        x_tok_in = [sem(f"x_tok_in{b}") for b in range(BATCH)]
        stats_consts_in, consts_in, weights_in, bias_in_sem = (
            sem("stats_consts_in"), sem("consts_in"), sem("weights_in"), sem("bias_in_sem"))
        ones_set, ones_b_set, eps_set = sem("ones_set"), sem("ones_b_set"), sem("eps_set")
        bias_split, bias_ready = sem("bias_split"), sem("bias_ready")
        raw1_done, chan1_done, centre1_done, mean1_done, spread1_done, var1_done, ln1_done, rstd1_done = (
            sem(n) for n in ("raw1_done", "chan1_done", "centre1_done", "mean1_done", "spread1_done",
                             "var1_done", "ln1_done", "rstd1_done"))
        rest1_done = sem("rest1_done")
        key_bias_done, fore_done, base_done = sem("key_bias_done"), sem("fore_done"), sem("base_done")
        pooled_done, f_done, fp_done, sq_done, norm2_done, lnorm_done, rnorm_done, key_done = (
            sem(n) for n in ("pooled_done", "f_done", "fp_done", "sq_done", "norm2_done", "lnorm_done",
                             "rnorm_done", "key_done"))
        score_done, kw_done, kw_copied, max_done, exp_done, rsum_done, att_done, attT_done, attT_copied = (
            sem(n) for n in ("score_done", "kw_done", "kw_copied", "max_done", "exp_done", "rsum_done",
                             "att_done", "attT_done", "attT_copied"))
        mix_done, x1_done = sem("mix_done"), sem("x1_done")
        raw2_done, chan2_done, centre2_done, mean2_done, spread2_done, var2_done, ln2_done, rstd2_done = (
            sem(n) for n in ("raw2_done", "chan2_done", "centre2_done", "mean2_done", "spread2_done",
                             "var2_done", "ln2_done", "rstd2_done"))
        rest2_done = sem("rest2_done")
        g_done, k_proj_done, q_proj_done, v_proj_done, ek_done, eq_done, phi_k_done, phi_q_done = (
            sem(n) for n in ("g_done", "k_proj_done", "q_proj_done", "v_proj_done", "ek_done", "eq_done",
                             "phi_k_done", "phi_q_done"))
        kd_done, kv_done, ksum_done, vsum_done, vsum_copied = (
            sem(n) for n in ("kd_done", "kv_done", "ksum_done", "vsum_done", "vsum_copied"))
        qk_done, den_done, den_read, z_done, zc_done, zT_done, vT_done, out_done, y_done, stored = (
            sem(n) for n in ("qk_done", "den_done", "den_read", "z_done", "zc_done", "zT_done", "vT_done", "out_done",
                             "y_done", "stored"))

        def in_order(steps):
            for step, image in steps:
                step(image)

        block = ctx.enter_context(nc.Block())

        @block.sync
        def _(sp):
            for b in range(BATCH):
                sp.dma_start(xT[:, b, :], x_chan[:, b, :]).then_inc(x_chan_in[b], 16)
            for b in range(BATCH):
                sp.dma_start(xt[:, b], x_tok[:, b]).then_inc(x_tok_in[b], 16)
            for b in range(BATCH):
                sp.wait_ge(y_done, b + 1)
                sp.dma_start(out[b], yT[:, b, :]).then_inc(stored, 16)
            sp.wait_ge(stored, 16 * BATCH)

        @block.gpsimd
        def _(pool):
            nc.gpsimd.memset(ones_b[:, :], 1.0).then_inc(ones_b_set, 1)
            nc.gpsimd.memset(ones[:, :], 1.0).then_inc(ones_set, 1)
            pool.dma_start(wts[:, :], weights).then_inc(weights_in, 16)
            pool.dma_start(bias_in[:, :], bias_rows).then_inc(bias_in_sem, 16)

            def split_biases():
                pool.wait_ge(bias_in_sem, 16)
                nc.gpsimd.tensor_copy(bias_parts[:, 0, :], bias_in[:, :]).then_inc(bias_split, 1)
                pool.wait_ge(bias_split, 1)
                nc.gpsimd.tensor_tensor(bias_rest[:, 0, :], bias_in[:, :], bias_parts[:, 0, :],
                                        ALU.subtract).then_inc(bias_split, 1)
                pool.wait_ge(bias_split, 2)
                nc.gpsimd.tensor_copy(bias_parts[:, 1, :], bias_rest[:, 0, :]).then_inc(bias_split, 1)
                pool.wait_ge(bias_split, 3)
                nc.gpsimd.tensor_tensor(bias_rest[:, 1, :], bias_rest[:, 0, :], bias_parts[:, 1, :],
                                        ALU.subtract).then_inc(bias_split, 1)
                pool.wait_ge(bias_split, 4)
                nc.gpsimd.tensor_copy(bias_parts[:, 2, :], bias_rest[:, 1, :]).then_inc(bias_split, 1)
                pool.wait_ge(bias_split, 5)
                for i in range(3):
                    nc.gpsimd.tensor_copy(bias[32 * i:32 * i + 32, :],
                                          bias_parts[32 * i:32 * i + 32, i, :]).then_inc(bias_ready, 1)

            split_biases()

        @block.scalar
        def _(act):
            act.dma_start(cst[:, 0:STATS_COLS], consts[:, 0:STATS_COLS]).then_inc(stats_consts_in, 16)
            act.dma_start(cst[:, STATS_COLS:], consts[:, STATS_COLS:]).then_inc(consts_in, 16)
            nc.scalar.preload_act_table_set("natural_log_exp_and_others")
            act.wait_ge(eps_set, 3)

            def rstd_first(b):
                some = part(b)
                act.wait_ge(var1_done, b + 1)
                nc.scalar.activation(lnvar1[:, some], VAR1[:, some], ACT.Ln, bias=eps[:, 0:1]).then_inc(ln1_done, 1)
                act.wait_ge(ln1_done, b + 1)
                nc.scalar.activation(rstd1[:, some], lnvar1[:, some], ACT.Exp,
                                     scale=-0.5).then_inc(rstd1_done, 1)

            def squares(b):
                act.wait_ge(x_chan_in[b], 16)
                act.wait_ge(key_bias_done, b + 1)
                nc.scalar.activation(sqT[:, b, :], xT[:, b, :], ACT.Square, bias=key_bias[:, b:b + 1],
                                     scale=rstd1[:, b:b + 1]).then_inc(sq_done, 1)

            def key_scale(b):
                act.wait_ge(norm2_done, b + 1)
                nc.scalar.activation(lnorm[:, b, :], NORM2, ACT.Ln).then_inc(lnorm_done, 1)
                act.wait_ge(lnorm_done, b + 1)
                nc.scalar.activation(rnorm[:, b, :], lnorm[:, b, :], ACT.Exp, scale=-0.5).then_inc(rnorm_done, 1)

            def exponentials(b):
                act.wait_ge(max_done, b + 1)
                for t in range(TT):
                    nc.scalar.activation(e[:, b, t, :], SCORE[:, t, :], ACT.Exp, bias=negmax[:, b, t:t + 1],
                                         accum_out=esum[:, b, t:t + 1]).then_inc(exp_done, 1)

            def copy_kw(b):
                act.wait_ge(kw_done, b + 1)
                nc.scalar.copy(kw[:, b].rearrange("p t c -> p (t c)"), KW).then_inc(kw_copied, 1)

            def copy_attT(b):
                act.wait_ge(attT_done, b + 1)
                nc.scalar.copy(attT[:, b].rearrange("p t q -> p (t q)"), ps_attT[:, :]).then_inc(attT_copied, 1)

            def rstd_second(b):
                act.wait_ge(var2_done, b + 1)
                nc.scalar.activation(lnvar2[:, b:b + 1], VAR2, ACT.Ln, bias=eps[:, 0:1]).then_inc(ln2_done, 1)
                act.wait_ge(ln2_done, b + 1)
                nc.scalar.activation(rstd2[:, b:b + 1], lnvar2[:, b:b + 1], ACT.Exp,
                                     scale=-0.5).then_inc(rstd2_done, 1)

            def exp_keys(b):
                act.wait_ge(k_proj_done, b + 1)
                nc.scalar.activation(ek[:, b, :], K1, ACT.Exp, bias=eps[:, 2:3]).then_inc(ek_done, 1)

            def exp_queries(b):
                act.wait_ge(q_proj_done, b + 1)
                nc.scalar.activation(eq[:, b, :], Q1, ACT.Exp, bias=eps[:, 2:3]).then_inc(eq_done, 1)

            def copy_vsum(b):
                act.wait_ge(vsum_done, b + 1)
                nc.scalar.copy(vsum[:, b, :], VSUM).then_inc(vsum_copied, 1)

            def widen_reciprocals(b):
                act.wait_ge(z_done, b + 1)
                nc.scalar.copy(zc[:, b].rearrange("p t (n d) -> p (t n) d", d=HD),
                               z[:, b, :].unsqueeze(2).to_broadcast([P, TT * HEADS, HD])).then_inc(zc_done, 1)

            in_order((
                (rstd_first, 0), (squares, 0), (key_scale, 0), (rstd_first, 1), (exponentials, 0), (squares, 1),
                (copy_kw, 0), (copy_attT, 0), (key_scale, 1), (squares, 2), (squares, 3), (copy_kw, 1),
                (key_scale, 2), (rstd_second, 0), (exponentials, 1), (copy_kw, 2), (exp_keys, 0), (exp_queries, 0),
                (copy_attT, 1), (copy_vsum, 0), (key_scale, 3), (widen_reciprocals, 0), (rstd_second, 1),
                (exponentials, 2), (exp_keys, 1), (exp_queries, 1), (copy_attT, 2), (copy_kw, 3),
                (exponentials, 3), (copy_vsum, 1), (rstd_second, 2), (copy_attT, 3), (exp_keys, 2),
                (widen_reciprocals, 1), (exp_queries, 2), (rstd_second, 3), (copy_vsum, 2), (exp_keys, 3),
                (widen_reciprocals, 2), (exp_queries, 3), (copy_vsum, 3), (widen_reciprocals, 3)))

        @block.vector
        def _(dve):
            for i, value in enumerate((GN_EPS, KEY_EPS, -1.0)):
                nc.vector.memset(eps[:, i:i + 1], value).then_inc(eps_set, 1)

            def channel_stats_first(b):
                some = part(b)
                for i in range(some.start, some.stop):
                    dve.wait_ge(x_chan_in[i], 16)
                    nc.vector.bn_stats(raw1[:, i, :], xT[:, i, :]).then_inc(raw1_done, 1)
                for i in range(some.start, some.stop):
                    dve.wait_ge(raw1_done, i + 1)
                    nc.vector.bn_aggr(chan1[:, i, :], raw1[:, i, :]).then_inc(chan1_done, 1)

            def group_stats_first(b):
                if b == 0:
                    dve.wait_ge(stats_consts_in, 16)
                some = part(b)
                dve.wait_ge(centre1_done, b + 1)
                nc.vector.tensor_tensor(rest1[:, some], chan1[:, some, 0], MEAN1[:, some],
                                        ALU.subtract).then_inc(rest1_done, 1)
                nc.vector.tensor_tensor(
                    mean1[:, :, some], MEAN1[:, some].unsqueeze(1).to_broadcast([P, 2, some.stop - some.start]),
                    const("signs").rearrange("p (s b) -> p s b", s=2)[:, :, some], ALU.mult).then_inc(mean1_done, 1)
                dve.wait_ge(rest1_done, b + 1)
                for i in range(some.start, some.stop):
                    nc.vector.scalar_tensor_tensor(spread1[:, i:i + 1], rest1[:, i:i + 1], rest1[:, i:i + 1],
                                                   chan1[:, i, 1:2], ALU.mult, ALU.add).then_inc(spread1_done, 1)

            def key_biases(b):
                some = part(b)
                dve.wait_ge(rstd1_done, b + 1)
                dve.wait_ge(mean1_done, b + 1)
                for i in range(some.start, some.stop):
                    nc.vector.tensor_scalar(key_bias[:, i:i + 1], mean1[:, 0, i:i + 1], rstd1[:, i:i + 1], KEY_EPS,
                                            ALU.mult, ALU.add).then_inc(key_bias_done, 1)

            def normalise_first(b):
                nc.vector.tensor_scalar(fT[:, b, :], xT[:, b, :], mean1[:, 0, b:b + 1], rstd1[:, b:b + 1],
                                        ALU.add, ALU.mult).then_inc(f_done, 1)
                dve.wait_ge(pooled_done, b + 1)
                nc.vector.tensor_scalar(fpT[:, b, :], POOLED[b], mean1[:, 1, b:b + 1], rstd1[:, b:b + 1],
                                        ALU.add, ALU.mult).then_inc(fp_done, 1)

            def base_of_mix(b):
                if b == 0:
                    dve.wait_ge(weights_in, 16)
                dve.wait_ge(fore_done, b + 1)
                nc.vector.scalar_tensor_tensor(base[:, b, :], BASE[b], weight("b_comb"), xT[:, b, :],
                                               ALU.add, ALU.add).then_inc(base_done, 1)

            def keys(b):
                dve.wait_ge(rnorm_done, b + 1)
                dve.wait_ge(f_done, b + 1)
                nc.vector.scalar_tensor_tensor(kT[:, b, :], fT[:, b, :], KEY_EPS, rnorm[:, b, :],
                                               ALU.add, ALU.mult).then_inc(key_done, 1)

            def row_max(b):
                dve.wait_ge(score_done, b + 1)
                nc.vector.tensor_reduce(negmax[:, b, :], SCORE, AX.X, ALU.max, negate=True).then_inc(max_done, 1)

            def normalise_att(b):
                dve.wait_ge(exp_done, TT * (b + 1))
                nc.vector.reciprocal(rsum[:, b, :], esum[:, b, :]).then_inc(rsum_done, 1)
                dve.wait_ge(rsum_done, b + 1)
                for t in range(TT):
                    nc.vector.tensor_scalar(att[:, b, t, :], e[:, b, t, :], rsum[:, b, t:t + 1], None,
                                            ALU.mult).then_inc(att_done, 1)

            def first_residual(b):
                dve.wait_ge(mix_done, b + 1)
                dve.wait_ge(base_done, b + 1)
                nc.vector.tensor_tensor(x1T[:, b, :], MIX, base[:, b, :], ALU.add).then_inc(x1_done, 1)
                dve.wait_ge(x1_done, b + 1)
                nc.vector.bn_stats(raw2[:, b, :], x1T[:, b, :]).then_inc(raw2_done, 1)
                dve.wait_ge(raw2_done, b + 1)
                nc.vector.bn_aggr(chan2[:, b, :], raw2[:, b, :]).then_inc(chan2_done, 1)

            def group_stats_second(b):
                dve.wait_ge(centre2_done, b + 1)
                nc.vector.tensor_tensor(rest2[:, b:b + 1], chan2[:, b, 0:1], MEAN2,
                                        ALU.subtract).then_inc(rest2_done, 1)
                nc.vector.tensor_copy(mean2[:, b:b + 1], MEAN2).then_inc(mean2_done, 1)
                dve.wait_ge(rest2_done, b + 1)
                nc.vector.scalar_tensor_tensor(spread2[:, b:b + 1], rest2[:, b:b + 1], rest2[:, b:b + 1],
                                               chan2[:, b, 1:2], ALU.mult, ALU.add).then_inc(spread2_done, 1)

            def normalise_second(b):
                dve.wait_ge(rstd2_done, b + 1)
                dve.wait_ge(mean2_done, b + 1)
                nc.vector.tensor_scalar(gT[:, b, :], x1T[:, b, :], mean2[:, b:b + 1], rstd2[:, b:b + 1],
                                        ALU.subtract, ALU.mult).then_inc(g_done, 1)

            def feature_map_keys(b):
                dve.wait_ge(ek_done, b + 1)
                nc.vector.scalar_tensor_tensor(phi_k[:, b, :], ek[:, b, :], 1.0, K1,
                                               ALU.min, ALU.max).then_inc(phi_k_done, 1)

            def feature_map_queries(b):
                dve.wait_ge(eq_done, b + 1)
                nc.vector.scalar_tensor_tensor(phi_q[:, b, :], eq[:, b, :], 1.0, Q1,
                                               ALU.min, ALU.max).then_inc(phi_q_done, 1)

            def values_times_keys(b):
                dve.wait_ge(phi_k_done, b + 1)
                nc.vector.tensor_reduce(kd[:, b, :], phi_k[:, b, :].rearrange("p (n d) -> p n d", d=HD),
                                        AX.X, ALU.add).then_inc(kd_done, 1)
                dve.wait_ge(kd_done, b + 1)
                dve.wait_ge(v_proj_done, b + 1)
                nc.vector.tensor_tensor(
                    kv[:, b].rearrange("p t (n d) -> p (t n) d", d=HD), V.rearrange("p (n d) -> p n d", d=HD),
                    kd[:, b, :].unsqueeze(2).to_broadcast([P, TT * HEADS, HD]), ALU.mult).then_inc(kv_done, 1)

            def query_times_sums(b):
                dve.wait_ge(phi_q_done, b + 1)
                dve.wait_ge(ksum_done, b + 1)
                nc.vector.tensor_tensor(
                    qk[:, b, :].rearrange("p (h w) -> p h w", w=W), phi_q[:, b, :].rearrange("p (h w) -> p h w", w=W),
                    KSUM.unsqueeze(2).to_broadcast([P, H, W]), ALU.mult).then_inc(qk_done, 1)

            def reciprocals(b):
                dve.wait_ge(den_done, b + 1)
                nc.vector.tensor_scalar(den[:, b, :], DEN, ATT_EPS, None, ALU.add).then_inc(den_read, 1)
                dve.wait_ge(den_read, b + 1)
                nc.vector.reciprocal(z[:, b, :], den[:, b, :]).then_inc(z_done, 1)

            def attended(b):
                dve.wait_ge(zT_done, b + 1)
                dve.wait_ge(vsum_copied, b + 1)
                nc.vector.tensor_tensor(
                    vT[:, b, :].rearrange("p (h w) -> p h w", w=W), ZT.rearrange("p (h w) -> p h w", w=W),
                    vsum[:, b, :].unsqueeze(2).to_broadcast([P, H, W]), ALU.mult).then_inc(vT_done, 1)

            def second_residual(b):
                dve.wait_ge(out_done, b + 1)
                nc.vector.scalar_tensor_tensor(yT[:, b, :], OUT, weight("bp"), x1T[:, b, :],
                                               ALU.add, ALU.add).then_inc(y_done, 1)

            in_order((
                (channel_stats_first, 0), (group_stats_first, 0), (key_biases, 0), (channel_stats_first, 1),
                (normalise_first, 0), (keys, 0), (group_stats_first, 1), (row_max, 0), (base_of_mix, 0),
                (key_biases, 1), (normalise_att, 0), (normalise_first, 1), (normalise_first, 2), (keys, 1),
                (first_residual, 0), (base_of_mix, 1), (base_of_mix, 2), (group_stats_second, 0), (keys, 2),
                (row_max, 1), (normalise_second, 0), (normalise_first, 3), (normalise_att, 1),
                (feature_map_keys, 0), (base_of_mix, 3), (values_times_keys, 0), (feature_map_queries, 0),
                (query_times_sums, 0), (first_residual, 1), (reciprocals, 0), (group_stats_second, 1), (keys, 3),
                (row_max, 2), (normalise_second, 1), (normalise_att, 2), (feature_map_keys, 1),
                (feature_map_queries, 1), (attended, 0), (values_times_keys, 1), (row_max, 3), (first_residual, 2),
                (query_times_sums, 1), (group_stats_second, 2), (normalise_att, 3), (reciprocals, 1),
                (normalise_second, 2), (second_residual, 0), (feature_map_keys, 2), (first_residual, 3),
                (feature_map_queries, 2), (values_times_keys, 2), (group_stats_second, 3), (query_times_sums, 2),
                (attended, 1), (normalise_second, 3), (second_residual, 1), (reciprocals, 2),
                (feature_map_keys, 3), (values_times_keys, 3), (feature_map_queries, 3), (query_times_sums, 3),
                (attended, 2), (reciprocals, 3), (second_residual, 2), (attended, 3), (second_residual, 3)))

        @block.tensor
        def _(pe):
            def stay_warm(count):
                for _ in range(count):
                    nc.tensor.matmul(ps_attT[:, 0:TOK], ones_b[:, 0:P], ones_b[:, :], start=True, stop=True)

            def stay_warm_last(count):
                pe.wait_ge(attT_copied, BATCH)
                stay_warm(count)

            def window_sums(b):
                if b == 0:
                    pe.wait_ge(consts_in, 16)
                pe.wait_ge(x_tok_in[b], 16)
                for t in range(TT):
                    first = t * (TOK - POOL_COLS)
                    mm = nc.tensor.matmul(POOLED[b][:, first:first + POOL_COLS], xt[:, b, t, :],
                                          const("window")[:, t * POOL_COLS:(t + 1) * POOL_COLS],
                                          start=(t == 0), stop=(t == TT - 1), skip_group_check=True)
                mm.then_inc(pooled_done, 1)

            def group_centre_first(b):
                if b == 0:
                    pe.wait_ge(stats_consts_in, 16)
                else:
                    pe.wait_ge(ln1_done, 1)
                some = part(b)
                pe.wait_ge(chan1_done, some.stop)
                nc.tensor.matmul(MEAN1[:, some], const("group_mean"), chan1[:, some, 0],
                                 start=True, stop=True).then_inc(centre1_done, 1)

            def group_var_first(b):
                some = part(b)
                pe.wait_ge(spread1_done, some.stop)
                pe.wait_ge(mean1_done, b + 1)
                nc.tensor.matmul(VAR1[:, some], const("group_mean"), spread1[:, some],
                                 start=True, stop=True).then_inc(var1_done, 1)

            def key_norms(b):
                if b == 0:
                    pe.wait_ge(ones_set, 1)
                pe.wait_ge(sq_done, b + 1)
                if b >= 1:
                    pe.wait_ge(kw_copied, b)
                nc.tensor.matmul(NORM2, ones[:, :], sqT[:, b, :], start=True, stop=True).then_inc(norm2_done, 1)

            def scores(b):
                pe.wait_ge(key_done, b + 1)
                pe.wait_ge(fp_done, b + 1)
                if b >= 1:
                    pe.wait_ge(exp_done, TT * b)
                for t in range(TT):
                    mm = nc.tensor.matmul(SCORE[:, t, :], fpT[:, b, t * P:(t + 1) * P], kT[:, b, :],
                                          start=True, stop=True)
                mm.then_inc(score_done, 1)

            def keys_recon(b):
                if b == 0:
                    pe.wait_ge(weights_in, 16)
                pe.wait_ge(key_done, b + 1)
                for t in range(TT):
                    mm = nc.tensor.matmul(KW[:, t * C:(t + 1) * C], kT[:, b, t * P:(t + 1) * P],
                                          weight("w_recon"), start=True, stop=True)
                mm.then_inc(kw_done, 1)

            def transpose_att(b):
                if b >= 1:
                    pe.wait_ge(attT_copied, b)
                for t in range(TT):
                    pe.wait_ge(att_done, TT * b + t + 1)
                    for s in range(TT):
                        mm = nc.tensor.transpose(ATTT[:, s, t * P:(t + 1) * P],
                                                 att[:, b, t, s * P:(s + 1) * P], const("identity"))
                mm.then_inc(attT_done, 1)

            def foreground(b):
                if b == 0:
                    pe.wait_ge(weights_in, 16)
                pe.wait_ge(fp_done, b + 1)
                nc.tensor.matmul(BASE[b], weight("w_fore"), fT[:, b, :], start=True, stop=True).then_inc(fore_done, 1)

            def mix(b):
                if b == 0:
                    pe.wait_ge(ln1_done, 2)
                else:
                    pe.wait_ge(x1_done, b)
                pe.wait_ge(kw_copied, b + 1)
                pe.wait_ge(attT_copied, b + 1)
                for t in range(TT):
                    mm = nc.tensor.matmul(MIX, kw[:, b, t, :], attT[:, b, t, :], start=(t == 0), stop=(t == TT - 1))
                mm.then_inc(mix_done, 1)

            def group_centre_second(b):
                pe.wait_ge(chan2_done, b + 1)
                if b == 0:
                    pe.wait_ge(base_done, 2)
                else:
                    pe.wait_ge(phi_q_done, b)
                nc.tensor.matmul(MEAN2, const("group_mean"), chan2[:, b, 0:1],
                                 start=True, stop=True).then_inc(centre2_done, 1)

            def group_var_second(b):
                pe.wait_ge(spread2_done, b + 1)
                pe.wait_ge(mean2_done, b + 1)
                nc.tensor.matmul(VAR2, const("group_mean"), spread2[:, b:b + 1],
                                 start=True, stop=True).then_inc(var2_done, 1)

            def project_keys(b):
                if b == 0:
                    pe.wait_ge(bias_ready, 3)
                    pe.wait_ge(base_done, 1)
                else:
                    pe.wait_ge(qk_done, b)
                pe.wait_ge(g_done, b + 1)
                for t in range(TT):
                    out_k = K1[:, t * C:(t + 1) * C]
                    nc.tensor.matmul(out_k, gT[:, b, t * P:(t + 1) * P], weight("wk"), start=True, stop=False)
                    mm = nc.tensor.matmul(out_k, ones_b[:, 0:P], bias[:, C:2 * C], start=False, stop=True)
                mm.then_inc(k_proj_done, 1)

            def project_values(b):
                if b == 0:
                    pe.wait_ge(bias_ready, 3)
                    pe.wait_ge(base_done, 3)
                else:
                    pe.wait_ge(den_read, b)
                pe.wait_ge(g_done, b + 1)
                for t in range(TT):
                    out_v = V[:, t * C:(t + 1) * C]
                    nc.tensor.matmul(out_v, gT[:, b, t * P:(t + 1) * P], weight("wv"), start=True, stop=False)
                    mm = nc.tensor.matmul(out_v, ones_b[:, 0:P], bias[:, 2 * C:3 * C], start=False, stop=True)
                mm.then_inc(v_proj_done, 1)

            def project_queries(b):
                if b == 0:
                    pe.wait_ge(bias_ready, 3)
                pe.wait_ge(g_done, b + 1)
                nc.tensor.matmul(Q1, weight("wq"), gT[:, b, :], start=True, stop=False)
                nc.tensor.matmul(Q1, bias[:, 0:C], ones_b[:, :], start=False, stop=True).then_inc(q_proj_done, 1)

            def row_sums_keys(b):
                pe.wait_ge(phi_k_done, b + 1)
                for t in range(TT):
                    mm = nc.tensor.matmul(KSUM[:, t * ROWS:(t + 1) * ROWS], phi_k[:, b, t * C:(t + 1) * C],
                                          const("blocks"), start=True, stop=True)
                mm.then_inc(ksum_done, 1)

            def row_sums_values(b):
                pe.wait_ge(kv_done, b + 1)
                for t in range(TT):
                    mm = nc.tensor.matmul(VSUM[:, t * ROWS:(t + 1) * ROWS], kv[:, b, t, :], const("blocks"),
                                          start=True, stop=True)
                mm.then_inc(vsum_done, 1)

            def denominators(b):
                pe.wait_ge(qk_done, b + 1)
                pe.wait_ge(vsum_copied, b + 1)
                for t in range(TT):
                    mm = nc.tensor.matmul(DEN[:, t * HEADS:(t + 1) * HEADS], qk[:, b, t * P:(t + 1) * P],
                                          const("blocks"), start=True, stop=True)
                mm.then_inc(den_done, 1)

            def spread_reciprocals(b):
                pe.wait_ge(zc_done, b + 1)
                if b == 0:
                    pe.wait_ge(base_done, BATCH)
                else:
                    pe.wait_ge(y_done, b)
                for t in range(TT):
                    mm = nc.tensor.transpose(ZT[:, t * P:(t + 1) * P], zc[:, b, t, :], const("identity"))
                mm.then_inc(zT_done, 1)

            def output_projection(b):
                pe.wait_ge(vT_done, b + 1)
                nc.tensor.matmul(OUT, weight("wp"), vT[:, b, :], start=True, stop=True).then_inc(out_done, 1)

            pe.wait_ge(ones_b_set, 1)
            in_order((
                (group_centre_first, 0), (stay_warm, 1), (group_var_first, 0), (stay_warm, 8), (window_sums, 0),
                (key_norms, 0), (stay_warm, 1), (group_centre_first, 1), (foreground, 0), (stay_warm, 2),
                (window_sums, 1), (scores, 0), (group_var_first, 1), (keys_recon, 0), (stay_warm, 2),
                (window_sums, 2), (stay_warm, 4), (window_sums, 3), (stay_warm, 1), (transpose_att, 0),
                (key_norms, 1), (foreground, 1), (mix, 0), (keys_recon, 1), (foreground, 2), (key_norms, 2),
                (group_centre_second, 0), (scores, 1), (group_var_second, 0), (keys_recon, 2), (project_keys, 0),
                (project_queries, 0), (foreground, 3), (transpose_att, 1), (project_values, 0), (row_sums_keys, 0),
                (mix, 1), (row_sums_values, 0), (key_norms, 3), (denominators, 0), (group_centre_second, 1),
                (scores, 2), (group_var_second, 1), (keys_recon, 3), (spread_reciprocals, 0), (project_keys, 1),
                (project_queries, 1), (project_values, 1), (transpose_att, 2), (scores, 3), (mix, 2),
                (row_sums_keys, 1), (row_sums_values, 1), (output_projection, 0), (group_centre_second, 2),
                (denominators, 1), (group_var_second, 2), (transpose_att, 3), (project_keys, 2), (mix, 3),
                (project_queries, 2), (stay_warm_last, 3), (project_values, 2), (group_centre_second, 3),
                (spread_reciprocals, 1), (row_sums_keys, 2), (stay_warm_last, 1), (group_var_second, 3),
                (row_sums_values, 2), (output_projection, 1), (denominators, 2), (project_keys, 3),
                (project_queries, 3), (project_values, 3), (row_sums_keys, 3), (spread_reciprocals, 2),
                (row_sums_values, 3), (denominators, 3), (output_projection, 2), (stay_warm_last, 2),
                (spread_reciprocals, 3), (stay_warm_last, 1), (output_projection, 3)))


def shape_constants():
    eye = np.eye(P, dtype=np.float32)
    same_group = np.kron(np.eye(P // GROUP, dtype=np.float32), np.ones((GROUP, GROUP), np.float32)) / GROUP
    signs = np.tile(np.array([[-1.0] * BATCH + [-9.0] * BATCH], np.float32), (P, 1))
    blocks = np.kron(np.eye(HEADS, dtype=np.float32), np.ones((HD, 1), np.float32))
    near = (np.abs(np.subtract.outer(np.arange(H), np.arange(H))) <= 1).astype(np.float32)
    line = near / near.sum(0) * 3.0
    full = np.kron(line, line)
    window = [full[t * P:(t + 1) * P, t * (TOK - POOL_COLS):t * (TOK - POOL_COLS) + POOL_COLS] for t in range(TT)]
    return np.ascontiguousarray(
        np.concatenate([same_group, signs, blocks, eye] + window, axis=1).astype(np.float32))


def kernel(x, L0_conv_mask, L0_conv_w_comb, L0_conv_b_comb, L1_conv_Wq, L1_conv_bq, L1_conv_Wk, L1_conv_bk,
           L1_conv_Wv, L1_conv_bv, L1_conv_Wp, L1_conv_bp):
    import concourse.bacc as bacc
    from concourse.bass_utils import run_bass_kernel_spmd

    images = np.asarray(x).reshape(BATCH, TOK, C)
    w_comb = np.asarray(L0_conv_w_comb)
    bias_rows = np.zeros((BIAS_ROWS, 3 * C), np.float32)
    for part in range(3):
        for i, row in enumerate((L1_conv_bq, L1_conv_bk, L1_conv_bv)):
            bias_rows[32 * part, i * C:(i + 1) * C] = np.asarray(row)
    bias_rows[1, 0:2 * C] = 1.0
    arrays = {
        "x_chan": np.ascontiguousarray(images.transpose(2, 0, 1)),
        "x_tok": np.ascontiguousarray(images.reshape(BATCH, TT, P, C).transpose(2, 0, 1, 3)),
        "consts": shape_constants(),
        "weights": np.ascontiguousarray(np.concatenate(
            [w_comb[0:C], w_comb[C:2 * C], np.asarray(L1_conv_Wq).T, np.asarray(L1_conv_Wk).T,
             np.asarray(L1_conv_Wv).T, np.asarray(L1_conv_Wp).T,
             np.asarray(L0_conv_b_comb)[:, None], np.asarray(L1_conv_bp)[:, None]], axis=1)),
        "bias_rows": bias_rows,
    }
    nc = bacc.Bacc("TRN2", target_bir_lowering=False, num_devices=1)
    args = [nc.dram_tensor(name, a.shape, F32, kind="ExternalInput").ap() for name, a in arrays.items()]
    out = nc.dram_tensor("out", (BATCH, C, TOK), F32, kind="ExternalOutput").ap()
    build_block(nc, *args, out)
    got = run_bass_kernel_spmd(nc, [arrays], core_ids=[0]).results[0]["out"]
    return np.ascontiguousarray(got.transpose(0, 2, 1)).reshape(BATCH, H, W, C)
```

```python
import numpy as np

import concourse.bass as bass
from concourse import mybir
from concourse.alu_op_type import AluOpType as ALU
from contextlib import ExitStack

F32 = mybir.dt.float32
BF16 = mybir.dt.bfloat16
ACT = mybir.ActivationFunctionType
AX = mybir.AxisListType

BATCH, H, W, C = 4, 16, 16, 128
TOK = H * W
P = 128
TT = TOK // P
GROUP = C // 32
HEADS = 8
HD = C // HEADS
ROWS = P // W
UNITS = BATCH - 1 + TT
POOL_COLS = (ROWS + 1) * W
BIAS_ROWS = 96
GN_EPS = 1e-5
KEY_EPS = 1e-7
ATT_EPS = 1e-6
QK = 2 * C

WEIGHTS = {}
for _name, _width in (("w_recon", C), ("w_fore", C), ("wq", C), ("wk", C), ("wv", C), ("wp", C),
                      ("b_comb", 1), ("bv", 1), ("bp", 1)):
    WEIGHTS[_name] = (sum(w for _, w in WEIGHTS.values()), _width)
WEIGHT_COLS = sum(w for _, w in WEIGHTS.values())

CONSTS = {}
for _name, _width in (("group_mean", P), ("signs", 2 * BATCH), ("window", TT * POOL_COLS),
                      ("identity", P), ("head_sum", P)):
    CONSTS[_name] = (sum(w for _, w in CONSTS.values()), _width)
CONST_COLS = sum(w for _, w in CONSTS.values())
STATS_COLS = CONSTS["window"][0]
WINDOW_END = CONSTS["identity"][0]


def build_block(nc, x_chan, x_tok, consts, weights, bias_rows, out):
    ctx = ExitStack()
    with ctx:
        def sb(name, shape, dt=F32):
            return ctx.enter_context(nc.sbuf_tensor(name, shape, dt))

        def psum(name):
            return ctx.enter_context(nc.psum_tensor(name, [P, 512], F32))

        def sem(name):
            return ctx.enter_context(nc.semaphore(name))

        xT = sb("xT", [P, BATCH, TOK])
        xt = sb("xt", [P, BATCH, TT, C])
        cst = sb("cst", [P, CONST_COLS])
        wts = sb("wts", [P, WEIGHT_COLS])
        bias_in = sb("bias_in", [BIAS_ROWS, QK])
        bias_rest = sb("bias_rest", [BIAS_ROWS, 2, QK])
        bias_parts = sb("bias_parts", [BIAS_ROWS, 3, QK], BF16)
        bias = sb("bias", [BIAS_ROWS, QK], BF16)
        ones = sb("ones", [P, P])
        ones_b = sb("ones_b", [BIAS_ROWS, TOK], BF16)
        eps = sb("eps", [P, 4])

        raw1 = sb("raw1", [P, BATCH, 6])
        chan1 = sb("chan1", [P, BATCH, 2])
        rest1 = sb("rest1", [P, BATCH])
        spread1 = sb("spread1", [P, BATCH])
        mean1 = sb("mean1", [P, 2, BATCH])
        key_bias = sb("key_bias", [P, BATCH])
        lnvar1 = sb("lnvar1", [P, BATCH])
        rstd1 = sb("rstd1", [P, BATCH])
        fT = sb("fT", [P, BATCH, TOK])
        fpT = sb("fpT", [P, BATCH, TOK])
        sqT = sb("sqT", [P, BATCH, TOK])
        lnorm = sb("lnorm", [P, BATCH, TOK])
        rnorm = sb("rnorm", [P, BATCH, TOK])
        kT = sb("kT", [P, BATCH, TOK])
        kw = sb("kw", [P, BATCH, TT, C])
        negmax = sb("negmax", [P, BATCH, TT])
        esum = sb("esum", [P, BATCH, TT])
        rsum = sb("rsum", [P, BATCH, TT])
        e = sb("e", [P, BATCH, TT, TOK])
        att = sb("att", [P, BATCH, TT, TOK])
        attT = sb("attT", [P, BATCH, TT, TOK])
        base = sb("base", [P, BATCH, TOK])
        x1T = sb("x1T", [P, BATCH, TOK])

        raw2 = sb("raw2", [P, BATCH, 6])
        chan2 = sb("chan2", [P, BATCH, 2])
        rest2 = sb("rest2", [P, BATCH])
        spread2 = sb("spread2", [P, BATCH])
        mean2 = sb("mean2", [P, BATCH])
        lnvar2 = sb("lnvar2", [P, BATCH])
        rstd2 = sb("rstd2", [P, BATCH])
        gT = sb("gT", [P, BATCH, TOK])
        ek = sb("ek", [P, BATCH, TOK])
        eq = sb("eq", [P, BATCH, TOK])
        phi_k = sb("phi_k", [P, BATCH, TOK])
        phi_q = sb("phi_q", [P, BATCH, TOK])
        ksum = sb("ksum", [P, BATCH, H])
        v = sb("v", [P, BATCH, TOK])
        kv = sb("kv", [P, BATCH, TOK])
        vsum = sb("vsum", [P, BATCH, H])
        qk = sb("qk", [P, BATCH, TOK])
        lnden = sb("lnden", [P, BATCH, TOK])
        z = sb("z", [P, BATCH, TOK])
        vT = sb("vT", [P, BATCH, TOK])
        yT = sb("yT", [P, BATCH, TOK])

        ps_pool = psum("ps_pool")
        ps_key = psum("ps_key")
        ps_score = psum("ps_score")
        ps_attT = psum("ps_attT")
        ps_mix = psum("ps_mix")
        ps_qk = psum("ps_qk")
        ps_v = psum("ps_v")
        ps_out = psum("ps_out")
        POOLED = [bank[:, 0:TOK] for bank in (ps_pool, ps_qk, ps_v, ps_out)]
        BASE = POOLED
        MEAN1, VAR1 = (ps_mix[:, TOK + BATCH * i:TOK + BATCH * (i + 1)] for i in range(2))
        NORM2 = ps_key[:, 0:TOK]
        KW = ps_key[:, TOK:2 * TOK]
        SCORE = ps_score[:, :].rearrange("p (t q) -> p t q", t=TT)
        ATTT = ps_attT[:, :].rearrange("p (t q) -> p t q", t=TT)
        MIX = ps_mix[:, 0:TOK]
        MEAN2, VAR2 = (ps_pool[:, TOK + i:TOK + i + 1] for i in range(2))
        K1 = [bank[:, 0:TOK] for bank in (ps_pool,) * BATCH + (ps_key,)]
        Q1 = ps_qk[:, 0:TOK]
        DEN = [bank[:, TOK:2 * TOK] for bank in (ps_qk,) * BATCH + (ps_mix,)]
        V = ps_v[:, 0:TOK]
        KD = ps_v[:, TOK:2 * TOK]
        OUT = [bank[:, 0:TOK] for bank in (ps_out,) * BATCH + (ps_score,)]

        def image(u):
            return min(u, BATCH - 1)

        def tokens(u):
            return slice(0, TOK) if u < BATCH - 1 else slice((u - BATCH + 1) * P, (u - BATCH + 2) * P)

        def rows(u):
            return slice(tokens(u).start // W, tokens(u).stop // W)

        def units_through(b):
            return b + 1 if b < BATCH - 1 else UNITS

        def part(b):
            return slice(0, 1) if b == 0 else slice(1, BATCH)

        def weight(name):
            a, n = WEIGHTS[name]
            return wts[:, a:a + n]

        def const(name):
            a, n = CONSTS[name]
            return cst[:, a:a + n]

        x_chan_in = [sem(f"x_chan_in{i}") for i in range(2)]
        x_tok_in = [sem(f"x_tok_in{i}") for i in range(2)]
        stats_consts_in, window_in, consts_in, weights_in, bias_in_sem = (
            sem(n) for n in ("stats_consts_in", "window_in", "consts_in", "weights_in", "bias_in_sem"))
        ones_set, ones_b_set, eps_set = sem("ones_set"), sem("ones_b_set"), sem("eps_set")
        bias_split, bias_ready = sem("bias_split"), sem("bias_ready")
        raw1_done, chan1_done, centre1_done, mean1_done, spread1_done, var1_done, ln1_done, rstd1_done = (
            sem(n) for n in ("raw1_done", "chan1_done", "centre1_done", "mean1_done", "spread1_done",
                             "var1_done", "ln1_done", "rstd1_done"))
        rest1_done = sem("rest1_done")
        key_bias_done, fore_done, base_done = sem("key_bias_done"), sem("fore_done"), sem("base_done")
        pooled_done, f_done, fp_done, sq_done, norm2_done, lnorm_done, rnorm_done, key_done = (
            sem(n) for n in ("pooled_done", "f_done", "fp_done", "sq_done", "norm2_done", "lnorm_done",
                             "rnorm_done", "key_done"))
        score_done, kw_done, kw_copied, max_done, exp_done, rsum_done, att_done, attT_done, attT_copied = (
            sem(n) for n in ("score_done", "kw_done", "kw_copied", "max_done", "exp_done", "rsum_done",
                             "att_done", "attT_done", "attT_copied"))
        mix_done, x1_done = sem("mix_done"), sem("x1_done")
        raw2_done, chan2_done, centre2_done, mean2_done, spread2_done, var2_done, ln2_done, rstd2_done = (
            sem(n) for n in ("raw2_done", "chan2_done", "centre2_done", "mean2_done", "spread2_done",
                             "var2_done", "ln2_done", "rstd2_done"))
        rest2_done = sem("rest2_done")
        g_done, k_proj_done, q_proj_done, v_proj_done, ek_done, eq_done, phi_k_done, phi_q_done = (
            sem(n) for n in ("g_done", "k_proj_done", "q_proj_done", "v_proj_done", "ek_done", "eq_done",
                             "phi_k_done", "phi_q_done"))
        ksum_done, v_done, kd_done, kv_done, vsum_done, qk_done = (
            sem(n) for n in ("ksum_done", "v_done", "kd_done", "kv_done", "vsum_done", "qk_done"))
        den_done, lnden_done, z_done, vT_done, out_done, y_done, stored = (
            sem(n) for n in ("den_done", "lnden_done", "z_done", "vT_done", "out_done", "y_done", "stored"))

        def in_order(steps):
            for step, n in steps:
                step(n)

        block = ctx.enter_context(nc.Block())

        @block.sync
        def _(sp):
            for i in range(2):
                images = part(i)
                sp.dma_start(xT[:, images, :], x_chan[:, images, :]).then_inc(x_chan_in[i], 16)
                sp.dma_start(xt[:, images], x_tok[:, images]).then_inc(x_tok_in[i], 16)
            sp.dma_start(wts[:, :], weights).then_inc(weights_in, 16)
            sp.dma_start(cst[:, WINDOW_END:], consts[:, WINDOW_END:]).then_inc(consts_in, 16)
            for u in range(UNITS):
                sp.wait_ge(y_done, u + 1)
                sp.dma_start(out[image(u)][:, tokens(u)], yT[:, image(u), tokens(u)]).then_inc(stored, 16)
            sp.wait_ge(stored, 16 * UNITS)

        @block.gpsimd
        def _(pool):
            nc.gpsimd.memset(ones[:, :], 1.0).then_inc(ones_set, 1)
            nc.gpsimd.memset(ones_b[:, :], 1.0).then_inc(ones_b_set, 1)
            pool.dma_start(bias_in[:, :], bias_rows).then_inc(bias_in_sem, 16)

            def split_biases():
                pool.wait_ge(bias_in_sem, 16)
                nc.gpsimd.tensor_copy(bias_parts[:, 0, :], bias_in[:, :]).then_inc(bias_split, 1)
                pool.wait_ge(bias_split, 1)
                nc.gpsimd.tensor_tensor(bias_rest[:, 0, :], bias_in[:, :], bias_parts[:, 0, :],
                                        ALU.subtract).then_inc(bias_split, 1)
                pool.wait_ge(bias_split, 2)
                nc.gpsimd.tensor_copy(bias_parts[:, 1, :], bias_rest[:, 0, :]).then_inc(bias_split, 1)
                pool.wait_ge(bias_split, 3)
                nc.gpsimd.tensor_tensor(bias_rest[:, 1, :], bias_rest[:, 0, :], bias_parts[:, 1, :],
                                        ALU.subtract).then_inc(bias_split, 1)
                pool.wait_ge(bias_split, 4)
                nc.gpsimd.tensor_copy(bias_parts[:, 2, :], bias_rest[:, 1, :]).then_inc(bias_split, 1)
                pool.wait_ge(bias_split, 5)
                for i in range(3):
                    nc.gpsimd.tensor_copy(bias[32 * i:32 * i + 32, :],
                                          bias_parts[32 * i:32 * i + 32, i, :]).then_inc(bias_ready, 1)

            split_biases()

        @block.scalar
        def _(act):
            act.dma_start(cst[:, 0:STATS_COLS], consts[:, 0:STATS_COLS]).then_inc(stats_consts_in, 16)
            act.dma_start(cst[:, STATS_COLS:WINDOW_END],
                          consts[:, STATS_COLS:WINDOW_END]).then_inc(window_in, 16)
            nc.scalar.preload_act_table_set("natural_log_exp_and_others")
            act.wait_ge(eps_set, 4)

            def rstd_first(b):
                some = part(b)
                act.wait_ge(var1_done, b + 1)
                nc.scalar.activation(lnvar1[:, some], VAR1[:, some], ACT.Ln, bias=eps[:, 0:1]).then_inc(ln1_done, 1)
                act.wait_ge(ln1_done, b + 1)
                nc.scalar.activation(rstd1[:, some], lnvar1[:, some], ACT.Exp,
                                     scale=-0.5).then_inc(rstd1_done, 1)

            def squares(b):
                act.wait_ge(x_chan_in[min(b, 1)], 16)
                act.wait_ge(key_bias_done, b + 1)
                nc.scalar.activation(sqT[:, b, :], xT[:, b, :], ACT.Square, bias=key_bias[:, b:b + 1],
                                     scale=rstd1[:, b:b + 1]).then_inc(sq_done, 1)

            def log_key_norm(b):
                act.wait_ge(norm2_done, b + 1)
                nc.scalar.activation(lnorm[:, b, :], NORM2, ACT.Ln).then_inc(lnorm_done, 1)

            def exp_key_scale(b):
                act.wait_ge(lnorm_done, b + 1)
                nc.scalar.activation(rnorm[:, b, :], lnorm[:, b, :], ACT.Exp, scale=-0.5).then_inc(rnorm_done, 1)

            def exponentials(b):
                act.wait_ge(max_done, b + 1)
                for t in range(TT):
                    nc.scalar.activation(e[:, b, t, :], SCORE[:, t, :], ACT.Exp, bias=negmax[:, b, t:t + 1],
                                         accum_out=esum[:, b, t:t + 1]).then_inc(exp_done, 1)

            def copy_kw(b):
                act.wait_ge(kw_done, b + 1)
                nc.scalar.copy(kw[:, b].rearrange("p t c -> p (t c)"), KW).then_inc(kw_copied, 1)

            def copy_attT(b):
                act.wait_ge(attT_done, b + 1)
                nc.scalar.copy(attT[:, b].rearrange("p t q -> p (t q)"), ps_attT[:, :]).then_inc(attT_copied, 1)

            def rstd_second(b):
                act.wait_ge(var2_done, b + 1)
                nc.scalar.activation(lnvar2[:, b:b + 1], VAR2, ACT.Ln, bias=eps[:, 0:1]).then_inc(ln2_done, 1)
                act.wait_ge(ln2_done, b + 1)
                nc.scalar.activation(rstd2[:, b:b + 1], lnvar2[:, b:b + 1], ACT.Exp,
                                     scale=-0.5).then_inc(rstd2_done, 1)

            def exp_keys(u):
                act.wait_ge(k_proj_done, u + 1)
                nc.scalar.activation(ek[:, image(u), tokens(u)], K1[u][:, tokens(u)], ACT.Exp,
                                     bias=eps[:, 2:3]).then_inc(ek_done, 1)

            def exp_queries(b):
                act.wait_ge(q_proj_done, b + 1)
                nc.scalar.activation(eq[:, b, :], Q1, ACT.Exp, bias=eps[:, 2:3]).then_inc(eq_done, 1)

            def values(b):
                if b == 0:
                    act.wait_ge(weights_in, 16)
                act.wait_ge(v_proj_done, b + 1)
                nc.scalar.activation(v[:, b, :], V, ACT.Identity, bias=weight("bv")).then_inc(v_done, 1)

            def log_denominators(u):
                b = image(u)
                act.wait_ge(den_done, u + 1)
                nc.scalar.activation(lnden[:, b, tokens(u)], DEN[u][:, tokens(u)], ACT.Ln,
                                     bias=eps[:, 3:4]).then_inc(lnden_done, 1)

            def exp_denominators(u):
                b = image(u)
                act.wait_ge(lnden_done, u + 1)
                nc.scalar.activation(z[:, b, tokens(u)], lnden[:, b, tokens(u)], ACT.Exp,
                                     scale=-1.0).then_inc(z_done, 1)

            in_order((
                (rstd_first, 0), (squares, 0), (log_key_norm, 0), (exp_key_scale, 0), (rstd_first, 1),
                (squares, 1), (copy_kw, 0), (exponentials, 0), (log_key_norm, 1), (exp_key_scale, 1), (squares, 2),
                (copy_attT, 0), (copy_kw, 1), (exponentials, 1), (log_key_norm, 2), (exp_key_scale, 2),
                (copy_attT, 1), (squares, 3), (rstd_second, 0), (copy_kw, 2), (exponentials, 2), (log_key_norm, 3),
                (exp_keys, 0), (exp_key_scale, 3), (values, 0), (exp_queries, 0), (copy_attT, 2), (rstd_second, 1),
                (log_denominators, 0), (exponentials, 3), (exp_keys, 1), (values, 1), (exp_denominators, 0),
                (exp_queries, 1), (copy_kw, 3), (copy_attT, 3), (rstd_second, 2), (log_denominators, 1),
                (exp_keys, 2), (exp_queries, 2), (exp_denominators, 1), (values, 2), (rstd_second, 3),
                (log_denominators, 2), (exp_denominators, 2), (exp_keys, 3), (exp_keys, 4), (exp_queries, 3),
                (values, 3), (log_denominators, 3), (log_denominators, 4), (exp_denominators, 3),
                (exp_denominators, 4)))

        @block.vector
        def _(dve):
            for i, value in enumerate((GN_EPS, KEY_EPS, -1.0, ATT_EPS)):
                nc.vector.memset(eps[:, i:i + 1], value).then_inc(eps_set, 1)

            def channel_stats_first(b):
                dve.wait_ge(x_chan_in[min(b, 1)], 16)
                nc.vector.bn_stats(raw1[:, b, :], xT[:, b, :]).then_inc(raw1_done, 1)

            def gather_stats_first(b):
                dve.wait_ge(raw1_done, b + 1)
                nc.vector.bn_aggr(chan1[:, b, :], raw1[:, b, :]).then_inc(chan1_done, 1)

            def group_stats_first(b):
                if b == 0:
                    dve.wait_ge(stats_consts_in, 16)
                some = part(b)
                dve.wait_ge(centre1_done, b + 1)
                nc.vector.tensor_tensor(rest1[:, some], chan1[:, some, 0], MEAN1[:, some],
                                        ALU.subtract).then_inc(rest1_done, 1)
                nc.vector.tensor_tensor(
                    mean1[:, :, some], MEAN1[:, some].unsqueeze(1).to_broadcast([P, 2, some.stop - some.start]),
                    const("signs").rearrange("p (s b) -> p s b", s=2)[:, :, some], ALU.mult).then_inc(mean1_done, 1)
                dve.wait_ge(rest1_done, b + 1)
                for i in range(some.start, some.stop):
                    nc.vector.scalar_tensor_tensor(spread1[:, i:i + 1], rest1[:, i:i + 1], rest1[:, i:i + 1],
                                                   chan1[:, i, 1:2], ALU.mult, ALU.add).then_inc(spread1_done, 1)

            def key_biases(b):
                dve.wait_ge(rstd1_done, min(b, 1) + 1)
                nc.vector.tensor_scalar(key_bias[:, b:b + 1], mean1[:, 0, b:b + 1], rstd1[:, b:b + 1], KEY_EPS,
                                        ALU.mult, ALU.add).then_inc(key_bias_done, 1)

            def normalise_first(b):
                dve.wait_ge(rstd1_done, min(b, 1) + 1)
                nc.vector.tensor_scalar(fT[:, b, :], xT[:, b, :], mean1[:, 0, b:b + 1], rstd1[:, b:b + 1],
                                        ALU.add, ALU.mult).then_inc(f_done, 1)

            def normalise_pooled(b):
                dve.wait_ge(rstd1_done, min(b, 1) + 1)
                dve.wait_ge(pooled_done, b + 1)
                nc.vector.tensor_scalar(fpT[:, b, :], POOLED[b], mean1[:, 1, b:b + 1], rstd1[:, b:b + 1],
                                        ALU.add, ALU.mult).then_inc(fp_done, 1)

            def base_of_mix(b):
                if b == 0:
                    dve.wait_ge(weights_in, 16)
                dve.wait_ge(fore_done, b + 1)
                nc.vector.scalar_tensor_tensor(base[:, b, :], BASE[b], weight("b_comb"), xT[:, b, :],
                                               ALU.add, ALU.add).then_inc(base_done, 1)

            def keys(b):
                dve.wait_ge(rnorm_done, b + 1)
                dve.wait_ge(f_done, b + 1)
                nc.vector.scalar_tensor_tensor(kT[:, b, :], fT[:, b, :], KEY_EPS, rnorm[:, b, :],
                                               ALU.add, ALU.mult).then_inc(key_done, 1)

            def row_max(b):
                dve.wait_ge(score_done, b + 1)
                nc.vector.tensor_reduce(negmax[:, b, :], SCORE, AX.X, ALU.max, negate=True).then_inc(max_done, 1)

            def reciprocal_sums(b):
                dve.wait_ge(exp_done, TT * (b + 1))
                nc.vector.reciprocal(rsum[:, b, :], esum[:, b, :]).then_inc(rsum_done, 1)

            def normalise_att(b):
                dve.wait_ge(rsum_done, b + 1)
                for t in range(TT):
                    nc.vector.tensor_scalar(att[:, b, t, :], e[:, b, t, :], rsum[:, b, t:t + 1], None,
                                            ALU.mult).then_inc(att_done, 1)

            def first_residual(b):
                dve.wait_ge(mix_done, b + 1)
                dve.wait_ge(base_done, b + 1)
                nc.vector.tensor_tensor(x1T[:, b, :], MIX, base[:, b, :], ALU.add).then_inc(x1_done, 1)

            def channel_stats_second(b):
                dve.wait_ge(x1_done, b + 1)
                nc.vector.bn_stats(raw2[:, b, :], x1T[:, b, :]).then_inc(raw2_done, 1)

            def gather_stats_second(b):
                dve.wait_ge(raw2_done, b + 1)
                nc.vector.bn_aggr(chan2[:, b, :], raw2[:, b, :]).then_inc(chan2_done, 1)

            def group_stats_second(b):
                dve.wait_ge(centre2_done, b + 1)
                nc.vector.tensor_tensor(rest2[:, b:b + 1], chan2[:, b, 0:1], MEAN2,
                                        ALU.subtract).then_inc(rest2_done, 1)
                nc.vector.tensor_copy(mean2[:, b:b + 1], MEAN2).then_inc(mean2_done, 1)

            def spread_second(b):
                dve.wait_ge(rest2_done, b + 1)
                nc.vector.scalar_tensor_tensor(spread2[:, b:b + 1], rest2[:, b:b + 1], rest2[:, b:b + 1],
                                               chan2[:, b, 1:2], ALU.mult, ALU.add).then_inc(spread2_done, 1)

            def normalise_second(u):
                b = image(u)
                dve.wait_ge(rstd2_done, b + 1)
                dve.wait_ge(mean2_done, b + 1)
                nc.vector.tensor_scalar(gT[:, b, tokens(u)], x1T[:, b, tokens(u)], mean2[:, b:b + 1], rstd2[:, b:b + 1],
                                        ALU.subtract, ALU.mult).then_inc(g_done, 1)

            def feature_map_keys(u):
                b = image(u)
                dve.wait_ge(ek_done, u + 1)
                nc.vector.scalar_tensor_tensor(phi_k[:, b, tokens(u)], ek[:, b, tokens(u)], 1.0, K1[u][:, tokens(u)],
                                               ALU.min, ALU.max).then_inc(phi_k_done, 1)

            def feature_map_queries(b):
                dve.wait_ge(eq_done, b + 1)
                nc.vector.scalar_tensor_tensor(phi_q[:, b, :], eq[:, b, :], 1.0, Q1,
                                               ALU.min, ALU.max).then_inc(phi_q_done, 1)

            def row_sums_keys(u):
                b = image(u)
                dve.wait_ge(phi_k_done, u + 1)
                nc.vector.tensor_reduce(ksum[:, b, rows(u)],
                                        phi_k[:, b, tokens(u)].rearrange("p (h w) -> p h w", w=W),
                                        AX.X, ALU.add).then_inc(ksum_done, 1)

            def values_times_keys(b):
                dve.wait_ge(v_done, b + 1)
                dve.wait_ge(kd_done, b + 1)
                nc.vector.tensor_tensor(kv[:, b, :], v[:, b, :], KD, ALU.mult).then_inc(kv_done, 1)

            def row_sums_values(b):
                dve.wait_ge(kv_done, b + 1)
                nc.vector.tensor_reduce(vsum[:, b, :], kv[:, b, :].rearrange("p (h w) -> p h w", w=W),
                                        AX.X, ALU.add).then_inc(vsum_done, 1)

            def by_sums(out_u, in_u, sums, u, done):
                b, count = image(u), rows(u).stop - rows(u).start
                nc.vector.tensor_tensor(
                    out_u[:, b, tokens(u)].rearrange("p (h w) -> p h w", w=W),
                    in_u[:, b, tokens(u)].rearrange("p (h w) -> p h w", w=W),
                    sums[:, b, rows(u)].unsqueeze(2).to_broadcast([P, count, W]), ALU.mult).then_inc(done, 1)

            def query_times_sums(u):
                dve.wait_ge(phi_q_done, image(u) + 1)
                dve.wait_ge(ksum_done, u + 1)
                by_sums(qk, phi_q, ksum, u, qk_done)

            def attended(u):
                dve.wait_ge(z_done, u + 1)
                dve.wait_ge(vsum_done, image(u) + 1)
                by_sums(vT, z, vsum, u, vT_done)

            def second_residual(u):
                b = image(u)
                dve.wait_ge(out_done, u + 1)
                nc.vector.scalar_tensor_tensor(yT[:, b, tokens(u)], OUT[u][:, tokens(u)], weight("bp"),
                                               x1T[:, b, tokens(u)], ALU.add, ALU.add).then_inc(y_done, 1)

            in_order((
                (channel_stats_first, 0), (gather_stats_first, 0), (group_stats_first, 0),
                (channel_stats_first, 1), (key_biases, 0), (gather_stats_first, 1), (channel_stats_first, 2),
                (normalise_first, 0), (channel_stats_first, 3), (gather_stats_first, 2), (gather_stats_first, 3),
                (normalise_pooled, 0), (group_stats_first, 1), (keys, 0), (key_biases, 1), (normalise_pooled, 1),
                (row_max, 0), (normalise_first, 1), (base_of_mix, 0), (key_biases, 2), (reciprocal_sums, 0),
                (normalise_att, 0), (keys, 1), (base_of_mix, 1), (key_biases, 3), (normalise_first, 2),
                (normalise_pooled, 2), (row_max, 1), (normalise_first, 3), (first_residual, 0),
                (channel_stats_second, 0), (reciprocal_sums, 1), (gather_stats_second, 0), (normalise_att, 1),
                (keys, 2), (group_stats_second, 0), (normalise_pooled, 3), (spread_second, 0), (base_of_mix, 2),
                (row_max, 2), (normalise_second, 0), (first_residual, 1), (reciprocal_sums, 2),
                (channel_stats_second, 1), (normalise_att, 2), (gather_stats_second, 1), (feature_map_keys, 0),
                (keys, 3), (row_sums_keys, 0), (group_stats_second, 1), (feature_map_queries, 0),
                (spread_second, 1), (query_times_sums, 0), (values_times_keys, 0), (row_max, 3),
                (normalise_second, 1), (row_sums_values, 0), (first_residual, 2), (channel_stats_second, 2),
                (reciprocal_sums, 3), (gather_stats_second, 2), (feature_map_keys, 1), (normalise_att, 3),
                (row_sums_keys, 1), (group_stats_second, 2), (feature_map_queries, 1), (spread_second, 2),
                (query_times_sums, 1), (values_times_keys, 1), (row_sums_values, 1), (normalise_second, 2),
                (base_of_mix, 3), (attended, 0), (first_residual, 3), (channel_stats_second, 3),
                (feature_map_keys, 2), (gather_stats_second, 3), (row_sums_keys, 2), (feature_map_queries, 2),
                (group_stats_second, 3), (spread_second, 3), (query_times_sums, 2), (attended, 1),
                (second_residual, 0), (normalise_second, 3), (normalise_second, 4), (values_times_keys, 2),
                (row_sums_values, 2), (feature_map_keys, 3), (attended, 2), (feature_map_keys, 4),
                (row_sums_keys, 3), (feature_map_queries, 3), (row_sums_keys, 4), (query_times_sums, 3),
                (query_times_sums, 4), (second_residual, 1), (values_times_keys, 3), (row_sums_values, 3),
                (second_residual, 2), (attended, 3), (attended, 4), (second_residual, 3), (second_residual, 4)))

        @block.tensor
        def _(pe):
            def stay_warm(count):
                for _ in range(count):
                    nc.tensor.matmul(ps_attT[:, 0:P], ones[:, :], ones[:, :], start=True, stop=True)

            def stay_warm_last(count):
                pe.wait_ge(attT_copied, BATCH)
                stay_warm(count)

            def window_sums(b):
                if b == 0:
                    pe.wait_ge(window_in, 16)
                pe.wait_ge(x_tok_in[min(b, 1)], 16)
                for t in range(TT):
                    first = t * (TOK - POOL_COLS)
                    mm = nc.tensor.matmul(POOLED[b][:, first:first + POOL_COLS], xt[:, b, t, :],
                                          const("window")[:, t * POOL_COLS:(t + 1) * POOL_COLS],
                                          start=(t == 0), stop=(t == TT - 1), skip_group_check=True)
                mm.then_inc(pooled_done, 1)

            def group_centre_first(b):
                if b == 0:
                    pe.wait_ge(stats_consts_in, 16)
                else:
                    pe.wait_ge(ln1_done, 1)
                some = part(b)
                pe.wait_ge(chan1_done, some.stop)
                nc.tensor.matmul(MEAN1[:, some], const("group_mean"), chan1[:, some, 0],
                                 start=True, stop=True).then_inc(centre1_done, 1)

            def group_var_first(b):
                some = part(b)
                pe.wait_ge(spread1_done, some.stop)
                pe.wait_ge(mean1_done, b + 1)
                nc.tensor.matmul(VAR1[:, some], const("group_mean"), spread1[:, some],
                                 start=True, stop=True).then_inc(var1_done, 1)

            def key_norms(b):
                pe.wait_ge(sq_done, b + 1)
                if b >= 1:
                    pe.wait_ge(kw_copied, b)
                nc.tensor.matmul(NORM2, ones[:, :], sqT[:, b, :], start=True, stop=True).then_inc(norm2_done, 1)

            def scores(b):
                pe.wait_ge(key_done, b + 1)
                pe.wait_ge(fp_done, b + 1)
                if b >= 1:
                    pe.wait_ge(exp_done, TT * b)
                for t in range(TT):
                    mm = nc.tensor.matmul(SCORE[:, t, :], fpT[:, b, t * P:(t + 1) * P], kT[:, b, :],
                                          start=True, stop=True)
                mm.then_inc(score_done, 1)

            def keys_recon(b):
                if b == 0:
                    pe.wait_ge(weights_in, 16)
                pe.wait_ge(key_done, b + 1)
                for t in range(TT):
                    mm = nc.tensor.matmul(KW[:, t * C:(t + 1) * C], kT[:, b, t * P:(t + 1) * P],
                                          weight("w_recon"), start=True, stop=True)
                mm.then_inc(kw_done, 1)

            def transpose_att(b):
                if b == 0:
                    pe.wait_ge(consts_in, 16)
                else:
                    pe.wait_ge(attT_copied, b)
                for t in range(TT):
                    pe.wait_ge(att_done, TT * b + t + 1)
                    for s in range(TT):
                        mm = nc.tensor.transpose(ATTT[:, s, t * P:(t + 1) * P],
                                                 att[:, b, t, s * P:(s + 1) * P], const("identity"))
                mm.then_inc(attT_done, 1)

            def foreground(b):
                if b == 0:
                    pe.wait_ge(weights_in, 16)
                pe.wait_ge(f_done, b + 1)
                pe.wait_ge(fp_done, b + 1)
                nc.tensor.matmul(BASE[b], weight("w_fore"), fT[:, b, :], start=True, stop=True).then_inc(fore_done, 1)

            def mix(b):
                if b == 0:
                    pe.wait_ge(ln1_done, 2)
                else:
                    pe.wait_ge(x1_done, b)
                pe.wait_ge(kw_copied, b + 1)
                pe.wait_ge(attT_copied, b + 1)
                for t in range(TT):
                    mm = nc.tensor.matmul(MIX, kw[:, b, t, :], attT[:, b, t, :], start=(t == 0), stop=(t == TT - 1))
                mm.then_inc(mix_done, 1)

            def group_centre_second(b):
                pe.wait_ge(chan2_done, b + 1)
                if b == 0:
                    pe.wait_ge(base_done, 1)
                else:
                    pe.wait_ge(phi_k_done, b)
                nc.tensor.matmul(MEAN2, const("group_mean"), chan2[:, b, 0:1],
                                 start=True, stop=True).then_inc(centre2_done, 1)

            def group_var_second(b):
                pe.wait_ge(spread2_done, b + 1)
                pe.wait_ge(mean2_done, b + 1)
                nc.tensor.matmul(VAR2, const("group_mean"), spread2[:, b:b + 1],
                                 start=True, stop=True).then_inc(var2_done, 1)

            def project_keys(u):
                b = image(u)
                if u == 0:
                    pe.wait_ge(ones_b_set, 1)
                    pe.wait_ge(bias_ready, 3)
                if u < BATCH:
                    pe.wait_ge(mean2_done, b + 1)
                    pe.wait_ge(ln2_done, b + 1)
                else:
                    pe.wait_ge(kw_copied, BATCH)
                out_k = K1[u][:, tokens(u)]
                nc.tensor.matmul(out_k, bias[:, C:2 * C], ones_b[:, tokens(u)], start=True, stop=False)
                pe.wait_ge(g_done, u + 1)
                nc.tensor.matmul(out_k, weight("wk"), gT[:, b, tokens(u)],
                                 start=False, stop=True).then_inc(k_proj_done, 1)

            def project_queries(b):
                if b == 0:
                    pe.wait_ge(ones_b_set, 1)
                    pe.wait_ge(bias_ready, 3)
                    pe.wait_ge(base_done, 2)
                else:
                    pe.wait_ge(phi_q_done, b)
                    pe.wait_ge(lnden_done, b)
                nc.tensor.matmul(Q1, bias[:, 0:C], ones_b[:, :], start=True, stop=False)
                pe.wait_ge(g_done, units_through(b))
                nc.tensor.matmul(Q1, weight("wq"), gT[:, b, :], start=False, stop=True).then_inc(q_proj_done, 1)

            def project_values(b):
                if b == 0:
                    pe.wait_ge(base_done, 3)
                else:
                    pe.wait_ge(kv_done, b)
                pe.wait_ge(g_done, units_through(b))
                nc.tensor.matmul(V, weight("wv"), gT[:, b, :], start=True, stop=True).then_inc(v_proj_done, 1)

            def head_sums_keys(b):
                if b == 0:
                    pe.wait_ge(consts_in, 16)
                pe.wait_ge(v_done, b + 1)
                pe.wait_ge(phi_k_done, units_through(b))
                nc.tensor.matmul(KD, const("head_sum"), phi_k[:, b, :], start=True, stop=True).then_inc(kd_done, 1)

            def denominators(u):
                if u == BATCH:
                    pe.wait_ge(x1_done, BATCH)
                pe.wait_ge(qk_done, u + 1)
                nc.tensor.matmul(DEN[u][:, tokens(u)], const("head_sum"), qk[:, image(u), tokens(u)],
                                 start=True, stop=True).then_inc(den_done, 1)

            def output_projection(u):
                if u == 0:
                    pe.wait_ge(base_done, BATCH)
                elif u < BATCH:
                    pe.wait_ge(y_done, u)
                else:
                    pe.wait_ge(exp_done, TT * BATCH)
                pe.wait_ge(vT_done, u + 1)
                nc.tensor.matmul(OUT[u][:, tokens(u)], weight("wp"), vT[:, image(u), tokens(u)],
                                 start=True, stop=True).then_inc(out_done, 1)

            pe.wait_ge(ones_set, 1)
            in_order((
                (stay_warm, 7), (group_centre_first, 0), (stay_warm, 2), (group_var_first, 0), (window_sums, 0),
                (stay_warm, 1), (key_norms, 0), (group_centre_first, 1), (window_sums, 1), (foreground, 0),
                (group_var_first, 1), (scores, 0), (keys_recon, 0), (key_norms, 1), (window_sums, 2),
                (foreground, 1), (transpose_att, 0), (scores, 1), (keys_recon, 1), (mix, 0), (key_norms, 2),
                (window_sums, 3), (foreground, 2), (group_centre_second, 0), (transpose_att, 1), (scores, 2),
                (group_var_second, 0), (keys_recon, 2), (mix, 1), (key_norms, 3), (project_keys, 0),
                (project_values, 0), (project_queries, 0), (transpose_att, 2), (group_centre_second, 1),
                (head_sums_keys, 0), (scores, 3), (group_var_second, 1), (denominators, 0), (mix, 2),
                (project_keys, 1), (project_values, 1), (project_queries, 1), (keys_recon, 3),
                (group_centre_second, 2), (head_sums_keys, 1), (transpose_att, 3), (foreground, 3),
                (group_var_second, 2), (denominators, 1), (mix, 3), (project_keys, 2), (project_queries, 2),
                (output_projection, 0), (group_centre_second, 3), (project_values, 2), (group_var_second, 3),
                (denominators, 2), (head_sums_keys, 2), (project_keys, 3), (project_keys, 4), (project_queries, 3),
                (project_values, 3), (output_projection, 1), (head_sums_keys, 3), (denominators, 3),
                (denominators, 4), (output_projection, 2), (output_projection, 3), (output_projection, 4)))


def shape_constants():
    eye = np.eye(P, dtype=np.float32)
    same_group = np.kron(np.eye(P // GROUP, dtype=np.float32), np.ones((GROUP, GROUP), np.float32)) / GROUP
    signs = np.tile(np.array([[-1.0] * BATCH + [-9.0] * BATCH], np.float32), (P, 1))
    head_sum = np.kron(np.eye(HEADS, dtype=np.float32), np.ones((HD, HD), np.float32))
    near = (np.abs(np.subtract.outer(np.arange(H), np.arange(H))) <= 1).astype(np.float32)
    line = near / near.sum(0) * 3.0
    full = np.kron(line, line)
    window = [full[t * P:(t + 1) * P, t * (TOK - POOL_COLS):t * (TOK - POOL_COLS) + POOL_COLS] for t in range(TT)]
    return np.ascontiguousarray(
        np.concatenate([same_group, signs] + window + [eye, head_sum], axis=1).astype(np.float32))


def kernel(x, L0_conv_mask, L0_conv_w_comb, L0_conv_b_comb, L1_conv_Wq, L1_conv_bq, L1_conv_Wk, L1_conv_bk,
           L1_conv_Wv, L1_conv_bv, L1_conv_Wp, L1_conv_bp):
    import concourse.bacc as bacc
    from concourse.bass_utils import run_bass_kernel_spmd

    images = np.asarray(x).reshape(BATCH, TOK, C)
    w_comb = np.asarray(L0_conv_w_comb)
    bias_rows = np.zeros((BIAS_ROWS, QK), np.float32)
    for part in range(3):
        for i, row in enumerate((L1_conv_bq, L1_conv_bk)):
            bias_rows[32 * part, i * C:(i + 1) * C] = np.asarray(row)
    bias_rows[1, :] = 1.0
    arrays = {
        "x_chan": np.ascontiguousarray(images.transpose(2, 0, 1)),
        "x_tok": np.ascontiguousarray(images.reshape(BATCH, TT, P, C).transpose(2, 0, 1, 3)),
        "consts": shape_constants(),
        "weights": np.ascontiguousarray(np.concatenate(
            [w_comb[0:C], w_comb[C:2 * C], np.asarray(L1_conv_Wq).T, np.asarray(L1_conv_Wk).T,
             np.asarray(L1_conv_Wv).T, np.asarray(L1_conv_Wp).T,
             np.asarray(L0_conv_b_comb)[:, None], np.asarray(L1_conv_bv)[:, None], np.asarray(L1_conv_bp)[:, None]], axis=1)),
        "bias_rows": bias_rows,
    }
    nc = bacc.Bacc("TRN2", target_bir_lowering=False, num_devices=1)
    args = [nc.dram_tensor(name, a.shape, F32, kind="ExternalInput").ap() for name, a in arrays.items()]
    out = nc.dram_tensor("out", (BATCH, C, TOK), F32, kind="ExternalOutput").ap()
    build_block(nc, *args, out)
    got = run_bass_kernel_spmd(nc, [arrays], core_ids=[0]).results[0]["out"]
    return np.ascontiguousarray(got.transpose(0, 2, 1)).reshape(BATCH, H, W, C)
```
